# Optimizing a Trainium2 kernel written in Bass

```python
import numpy as np
import jax
import jax.numpy as jnp

def _softmax(x, axis=-1):
    return jax.nn.softmax(x, axis=axis)

def _gelu(x):
    return jax.nn.gelu(x, approximate=True)

def _silu(x):
    return jax.nn.silu(x)

def _sigmoid(x):
    return jax.nn.sigmoid(x)

def _layernorm(x, axis=-1, eps=1e-05):
    m = jnp.mean(x, axis=axis, keepdims=True)
    v = jnp.var(x, axis=axis, keepdims=True)
    return (x - m) / jnp.sqrt(v + eps)

def _scatter_add(tgt, idx, src, axis=0):
    return tgt.at[idx].add(src)

def _segment_sum(src, seg, n):
    return jax.ops.segment_sum(src, seg, n)
kernel_name = 'mk_seq_postln_d1_jaxref_r8_eb6085'

def setup_inputs(seed: int=0):
    np.random.seed(seed)
    _w = jnp.asarray

    def _L0_attn_setup():
        import jax, jax.numpy as jnp
        import numpy as np
        MAX_DIST = 8
        GUIDANCE_WEIGHT = 0.4
        EPS_MAG = 1e-06
        EPS_COS = 1e-08
        EPS_WSUM = 1e-08
        key = jax.random.key(seed)
        k1, k2 = jax.random.split(key)
        embeddings = jax.random.normal(k1, (4, 256, 128), dtype=jnp.float32)
        guidance_trajectories = jax.random.normal(k2, (64, 128), dtype=jnp.float32)
        return {'embeddings': embeddings, 'guidance_trajectories': guidance_trajectories}
    _L0_attn_in = _L0_attn_setup()

    def _L0_ffn_setup():
        import jax, jax.numpy as jnp
        import numpy as np
        B, S, D, F, E = (4, 256, 128, 512, 8)
        LN_EPS = 1e-05
        key = jax.random.key(seed)
        ks = jax.random.split(key, 6)
        sc = 0.02
        return {'x': jax.random.normal(ks[0], (B, S, D), dtype=jnp.float32), 'Wr': jax.random.normal(ks[1], (D, E), dtype=jnp.float32) * sc, 'br': jnp.zeros((E,), jnp.float32), 'ln_g': jnp.ones((D,), jnp.float32), 'ln_b': jnp.zeros((D,), jnp.float32), 'W1': jax.random.normal(ks[2], (E, D, F), dtype=jnp.float32) * sc, 'b1': jnp.zeros((E, F), jnp.float32), 'W2': jax.random.normal(ks[3], (E, F, D), dtype=jnp.float32) * sc, 'b2': jnp.zeros((E, D), jnp.float32)}
    _L0_ffn_in = _L0_ffn_setup()
    _d = {'L0_attn_embeddings': _L0_attn_in['embeddings'], 'L0_attn_guidance_trajectories': _L0_attn_in['guidance_trajectories'], 'L0_ffn_Wr': _L0_ffn_in['Wr'], 'L0_ffn_br': _L0_ffn_in['br'], 'L0_ffn_ln_g': _L0_ffn_in['ln_g'], 'L0_ffn_ln_b': _L0_ffn_in['ln_b'], 'L0_ffn_W1': _L0_ffn_in['W1'], 'L0_ffn_b1': _L0_ffn_in['b1'], 'L0_ffn_W2': _L0_ffn_in['W2'], 'L0_ffn_b2': _L0_ffn_in['b2']}
    _x0 = _d['L0_attn_embeddings']
    _d['L0_attn_embeddings'] = jax.random.normal(jax.random.fold_in(jax.random.key(seed), 1), (16, 256, 128), dtype=_x0.dtype)
    del _x0
    return _d

def reference(L0_attn_embeddings, L0_attn_guidance_trajectories, L0_ffn_Wr, L0_ffn_br, L0_ffn_ln_g, L0_ffn_ln_b, L0_ffn_W1, L0_ffn_b1, L0_ffn_W2, L0_ffn_b2):

    def _L0_attn_ref(embeddings, guidance_trajectories):
        import jax, jax.numpy as jnp
        import numpy as np
        MAX_DIST = 8
        GUIDANCE_WEIGHT = 0.4
        EPS_MAG = 1e-06
        EPS_COS = 1e-08
        EPS_WSUM = 1e-08
        B, S, D = embeddings.shape
        W = min(MAX_DIST, S - 1)
        diffs = embeddings[:, 1:, :] - embeddings[:, :-1, :]
        pos = jnp.arange(S)[:, None]
        k = jnp.arange(W)[None, :]
        idx = pos - W + k
        valid = (idx >= 0) & (pos >= 1)
        windows = diffs[:, jnp.clip(idx, 0, S - 2), :]
        w = jnp.minimum(pos, W)
        j = k - (W - w)
        lin = jnp.where(w > 1, 0.1 + 0.9 * j / jnp.maximum(w - 1, 1), 0.1)
        pos_weights = jnp.where(valid, lin, 0.0).astype(embeddings.dtype)
        mag = jnp.linalg.norm(windows, axis=-1, keepdims=True)
        is_valid_mag = mag > EPS_MAG
        normed = jnp.where(is_valid_mag, windows / jnp.where(is_valid_mag, mag, 1.0), 0.0)
        mag_weights = jnp.tanh(mag * 2.0)
        combined = pos_weights[None, :, :, None] * mag_weights
        g_norm = jnp.linalg.norm(guidance_trajectories, axis=-1)
        a_norm = jnp.linalg.norm(normed, axis=-1)
        dots = jnp.einsum('bswd,gd->bswg', normed, guidance_trajectories)
        sims = dots / (jnp.maximum(a_norm, EPS_COS)[..., None] * jnp.maximum(g_norm, EPS_COS))
        g_weights = jax.nn.softmax(sims * 2.0, axis=-1)
        influence = jnp.einsum('bswg,gd->bswd', g_weights, guidance_trajectories)
        blended = (1.0 - GUIDANCE_WEIGHT) * normed + GUIDANCE_WEIGHT * influence
        weight_sum = jnp.maximum(combined.sum(axis=2), EPS_WSUM)
        trajectories = (blended * combined).sum(axis=2) / weight_sum
        return trajectories

    def _L0_ffn_ref(x, Wr, br, ln_g, ln_b, W1, b1, W2, b2):
        import jax, jax.numpy as jnp
        import numpy as np
        B, S, D, F, E = (4, 256, 128, 512, 8)
        LN_EPS = 1e-05
        tokens_shape = x.shape[:-1]
        xt = x.reshape(-1, x.shape[-1])
        router_logits = xt @ Wr + br
        router_probs = jax.nn.softmax(router_logits, axis=-1)
        gates = jnp.max(router_probs, axis=-1, keepdims=True)
        idx = jnp.argmax(router_probs, axis=-1)
        onehot = jax.nn.one_hot(idx, E, dtype=xt.dtype)
        mu = jnp.mean(xt, axis=-1, keepdims=True)
        var = jnp.mean(jnp.square(xt - mu), axis=-1, keepdims=True)
        xn = (xt - mu) * jax.lax.rsqrt(var + LN_EPS) * ln_g + ln_b
        h = jnp.einsum('te,td,edf->tf', onehot, xn, W1) + b1[idx]
        h = jax.nn.relu(h)
        y = jnp.einsum('te,tf,efd->td', onehot, h, W2) + b2[idx]
        y = y * gates
        return y.reshape(tokens_shape + (y.shape[-1],))
    x = L0_attn_embeddings
    x = _layernorm(x + _L0_attn_ref(x, L0_attn_guidance_trajectories), axis=-1)
    x = _layernorm(x + _L0_ffn_ref(x, L0_ffn_Wr, L0_ffn_br, L0_ffn_ln_g, L0_ffn_ln_b, L0_ffn_W1, L0_ffn_b1, L0_ffn_W2, L0_ffn_b2), axis=-1)
    return x

_drawn_inputs = setup_inputs


def setup_inputs(seed=0):
    import zlib

    import numpy as np

    out = dict(_drawn_inputs(seed))
    spreads = {'L0_ffn_br': (0.0, 0.376),
     'L0_ffn_ln_g': (1.0, 0.6),
     'L0_ffn_ln_b': (0.0, 0.8),
     'L0_ffn_b1': (0.0, 0.8),
     'L0_ffn_b2': (0.0, 0.463)}
    factors = {'L0_ffn_Wr': 2.717, 'L0_ffn_W1': 4.831, 'L0_ffn_W2': 3.854}
    for name, (base, spread) in spreads.items():
        noise = np.random.default_rng([zlib.crc32(name.encode()), seed]).standard_normal(out[name].shape)
        drawn = base * np.exp(spread * noise) if base else spread * noise
        out[name] = jnp.asarray(drawn.astype(out[name].dtype))
    for name, factor in factors.items():
        out[name] = (out[name] * factor).astype(out[name].dtype)
    return out
```

```python
from contextlib import ExitStack

import numpy as np

import concourse.bass as bass
from concourse import mybir

F32 = mybir.dt.float32
F16 = mybir.dt.float16
BF16 = mybir.dt.bfloat16
I32 = mybir.dt.int32
ALU = mybir.AluOpType
ACT = mybir.ActivationFunctionType
AX = mybir.AxisListType

P = 128
B, S, D = 16, 256, 128
T = B * S
E, FF = 8, 512
FC = FF // P
G = 64
W = 8
NT = 4
NU = T // (NT * P)
REG = T + P
PADROW = E * REG
NB = (T + E * (P - 1)) // P
ROW = D + 4
UN = 6
LN_EPS = 1e-5
EPS_MAG, EPS_COS, EPS_WSUM, GUIDE = 1e-6, 1e-8, 1e-8, 0.4
POW2_MASK = 0x7F800000

C_BAND = 0
C_ID = C_BAND + 4 * P
C_LT = C_ID + P
C_REG = C_LT + P
C_REV = C_REG + E
C_BLK = C_REV + E
C_TOK = C_BLK + NB
C_EID = C_TOK + NU * NT
C_N = C_EID + 1


def constants():
    c = np.zeros((P, C_N), np.float32)
    for s in range(1, S):
        w = min(s, W)
        for j in range(w):
            i = s - w + j
            v = np.float32(0.1) + np.float32(0.9) * np.float32(j) / np.float32(max(w - 1, 1)) if w > 1 else 0.1
            c[i // 2, C_BAND + (2 * (i % 2) + s % 2) * P + s // 2] = v
    c[:, C_ID:C_ID + P] = np.eye(P)
    c[:, C_LT:C_LT + P] = np.triu(np.ones((P, P)), 1)
    c[:, C_REG:C_REG + E] = np.arange(E) * REG
    c[:, C_REV:C_REV + E] = E - np.arange(E)
    c[:, C_BLK:C_BLK + NB] = np.arange(NB)
    p = np.arange(P)
    for u in range(NU):
        for k in range(NT):
            c[:, C_TOK + u * NT + k] = (2 * u + k // 2) * S + 2 * p + k % 2
    c[:, C_EID] = np.where((p % 32 < E) & (p < 96), p % 32, -1)
    return c


def build(nc, x, guide, wr, br, ln_g, ln_b, w1, b1, w2, b2, cst, rows, out):
    with ExitStack() as ctx:
        def sb(name, shape, dt=F32):
            return ctx.enter_context(nc.sbuf_tensor(name, shape, dt))

        def sem(name):
            return ctx.enter_context(nc.semaphore(name))

        bank = [ctx.enter_context(nc.psum_tensor(f"bank{i}", [P, 512], F32)) for i in range(8)]

        C = sb("C", [P, C_N])
        lt16 = sb("lt16", [P, P], BF16)
        ones16 = sb("ones16", [P, P], BF16)
        ones = sb("ones", [P, P])
        gd = sb("gd", [G, D])
        gdn = sb("gdn", [G, D])
        gdT = sb("gdT", [P, G])
        gdz = sb("gdz", [G, D + 1])
        gst = sb("gst", [G, 4])
        epsc = sb("epsc", [P, 1])
        Wr = sb("Wr", [P, E])
        brb = sb("brb", [P, E])
        gb = sb("gb", [P, 2])
        gbs = sb("gbs", [P, 2])
        W1 = sb("W1", [P, E, FF])
        W2 = sb("W2", [P, E, FC, D])
        W1h = sb("W1h", [P, E * FF], F16)
        W1l = sb("W1l", [P, E * FF], F16)
        W2hl = sb("W2hl", [P, E * FC, 2 * D], F16)
        bias = sb("bias", [96, FF + D])
        bias_r = sb("bias_r", [96, FF + D])
        bias_h = sb("bias_h", [96, FF + D], BF16)
        bias_m = sb("bias_m", [96, FF + D], BF16)
        bias_l = sb("bias_l", [96, FF + D], BF16)
        bias3 = sb("bias3", [96, FF + D], BF16)
        mx = sb("mx", [P, 16])
        mx4 = sb("mx4", [4, 8])
        scl = sb("scl", [P, 16])

        X = sb("X", [P, B, 2, D])
        XN = sb("XN", [P, B, D])
        Dd = [sb(f"Dd{i}", [P, 2, 2, D]) for i in range(2)]
        sq = sb("sq", [P, D])
        N = [sb(f"N{i}", [P, NT, D]) for i in range(2)]
        V = [sb(f"V{i}", [P, NT, D + 1]) for i in range(3)]
        nT = sb("nT", [P, NT * P])
        ET = [sb(f"ET{i}", [G, NT * P]) for i in range(2)]
        pin = [sb(f"pin{i}", [P, 12]) for i in range(2)]
        prt = [sb(f"prt{i}", [P, 12]) for i in range(2)]
        pgd = sb("pgd", [P, 12])
        half12 = sb("half12", [P, 12])
        st = [sb(f"st{i}", [P, 12, NT]) for i in range(3)]
        Y = sb("Y", [P, NT, D])
        bn = sb("bn", [P, NT, 6])
        mv = [sb(f"mv{i}", [P, NT, 2]) for i in range(2)]
        R = [sb(f"R{i}", [P, NT, ROW]) for i in range(4)]
        xT = sb("xT", [P, NT * P])
        lg = sb("lg", [P, NT, E])
        ex = sb("ex", [P, NT, E])
        oh = sb("oh", [P, NT, E])
        oh16 = sb("oh16", [P, NT, E], BF16)
        carry = sb("carry", [P, E])
        carry16 = sb("carry16", [P, E], BF16)
        rt = sb("rt", [P, 4, NT])
        place = [sb(f"place{i}", [P, NT], I32) for i in range(4)]

        tot = sb("tot", [P, E])
        nblk = sb("nblk", [P, E])
        nblk_i = sb("nblk_i", [P, E], I32)
        pl = sb("pl", [P, NT, E])
        cnt = sb("cnt", [P, E])
        cend = sb("cend", [P, E])
        jump = sb("jump", [P, E])
        past = sb("past", [P, NB, E])
        past2 = sb("past2", [P, NB, E])
        blk = sb("blk", [P, 3, NB])
        blk_e = sb("blk_e", [P, NB], I32)
        blk_row = sb("blk_row", [P, NB], I32)
        pad_row = sb("pad_row", [P, E], I32)
        sel16 = sb("sel16", [96, NB], BF16)
        padt = sb("padt", [P, ROW])

        XR = [sb(f"XR{i}", [P, ROW]) for i in range(UN)]
        xs = [sb(f"xs{i}", [P, D]) for i in range(UN)]
        cg = [sb(f"cg{i}", [P, 1]) for i in range(UN)]
        xt = [sb(f"xt{i}", [P, P]) for i in range(UN)]
        xh = [sb(f"xh{i}", [P, P], F16) for i in range(UN)]
        xl = [sb(f"xl{i}", [P, P], F16) for i in range(UN)]
        hh = [sb(f"hh{i}", [P, FF], F16) for i in range(UN)]
        hl = [sb(f"hl{i}", [P, FF], F16) for i in range(UN)]
        z0 = sb("zpart", [P, D])
        z = [sb(f"z{i}", [P, D]) for i in range(UN)]
        bn2 = sb("bn2", [P, 6])
        mv2 = [sb(f"mv2{i}", [P, 2]) for i in range(UN)]
        sd = [sb(f"sd{i}", [P, 2]) for i in range(UN)]
        OUT = [sb(f"OUT{i}", [P, D]) for i in range(UN)]

        ld = {n: sem("ld_" + n) for n in ("cst", "guide", "small", "x0", "x1", "x2", "x3", "w1", "w2", "bias")}
        names = ("zeroed diff sumsq moments_in guarded roots mags tanh scales n np nT_ps nT_sb sims_ps ET "
                 "infl_ps V traj_ps y mvd roots2 x1c x1 xT_ps xT_sb logits_ps shifted exped onehot rank_ps placed "
                 "counted guide_sq guide_norm guided guideT_ps guideT split_hi split_lo maxima maxT_ps max4 maxb_ps scales_w "
                 "bias3 tot_ps table pads_ready").split()
        s = {n: sem(n) for n in names}
        scattered = [sem(f"scattered{i}") for i in range(4)]
        padded = sem("padded")
        names2 = "b_xs b_xT_ps b_xt b_xh b_xl b_h_ps b_hh b_hl b_y_ps b_z b_mv b_sd b_out b_rec".split()
        t = {n: sem(n) for n in names2}
        seen = sem("seen")
        row_loaded = [sem(f"row_loaded{i}") for i in range(UN)]
        stored = [sem(f"stored{i}") for i in range(UN)]

        band = [[C[:, C_BAND + (2 * a + b) * P:C_BAND + (2 * a + b + 1) * P] for b in range(2)] for a in range(2)]
        ident = C[:, C_ID:C_ID + P]
        nT_ps, sims_ps = bank[0], bank[1]
        infl_ps, traj_ps, xT_ps, log_ps = [bank[2], bank[3]], [bank[4], bank[5]], bank[6], bank[7]
        rank_ps = log_ps[:, 64:64 + NT * E]

        def half(banks, k):
            return banks[k // 2][:, (k % 2) * (D + 1):(k % 2 + 1) * (D + 1)]

        def pair(b):
            return b[:, 0:2 * (D + 1)].rearrange("p (k d) -> p k d", k=2)

        block = ctx.enter_context(nc.Block())

        MAG, MAGC, INV, CN, MT, Q, ZI, WI, R1, SS, VP, WR = range(12)

        def after(eng, signal, count):
            if not isinstance(count, int) or count > 0:
                eng.wait_ge(signal, count)

        def steps(eng, stages):
            lo = min(l for l, _ in stages)
            hi = max(l for l, _ in stages)
            def at(b0, turn, k):
                for lead, f in stages:
                    q = k + lead
                    if b0 + q >= 0:
                        f(turn + q // UN, q % UN)
            for b in range(-hi, 0):
                for lead, f in stages:
                    if b + lead >= 0:
                        f(0, b + lead)
            for k in range(UN):
                at(0, 0, k)
            n = (NB - hi) // UN
            with eng.Fori(1, n) as turn:
                for k in range(UN):
                    at(UN, turn, k)
            for b in range(n * UN, NB - lo):
                for lead, f in stages:
                    if 0 <= b + lead < NB:
                        f((b + lead) // UN, (b + lead) % UN)

        @block.sync
        def _(sp):
            sp.dma_start(X[:, 0:2, :, :], x[0:2].rearrange("b (p c) d -> p b (c d)", c=2).rearrange(
                "p b (c d) -> p b c d", c=2)).then_inc(ld["x0"], 16)
            nxt = x.rearrange("b s d -> (b s) d")
            nv = nxt[2:T, :].rearrange("(n c) d -> n c d", c=2)[:, 0, :]
            def next_rows(b0, b1, which):
                if b1 < B:
                    sp.dma_start(XN[:, b0:b1, :], nv[b0 * P:b1 * P, :].rearrange("(b p) d -> p b d", p=P)).then_inc(ld[which], 16)
                else:
                    sp.dma_start(XN[:, b0:B - 1, :], nv[b0 * P:(B - 1) * P, :].rearrange("(b p) d -> p b d", p=P)).then_inc(ld[which], 16)
                    sp.dma_start(XN[0:P - 1, B - 1, :], nv[(B - 1) * P:B * P - 1, :]).then_inc(ld[which], 16)
                    sp.dma_start(XN[P - 1:P, B - 1, :], nxt[T - 1:T, :]).then_inc(ld[which], 16)
            next_rows(0, 2, "x0")
            sp.dma_start(C[:, :], cst).then_inc(ld["cst"], 16)
            for n, (a, b) in enumerate(((2, 6), (6, 10), (10, 16)), 1):
                sp.dma_start(X[:, a:b, :, :], x[a:b].rearrange("b (p c) d -> p b c d", c=2)).then_inc(ld[f"x{n}"], 16)
                next_rows(a, b, f"x{n}")
            sp.dma_start(W1[:, :, :], w1.rearrange("e d f -> d e f")).then_inc(ld["w1"], 16)
            sp.dma_start(W2[:, :, :, :], w2.rearrange("e (c p) d -> p e c d", p=P)).then_inc(ld["w2"], 16)
            sp.wait_ge(s["pads_ready"], 1)
            sp.dma_start(rows[PADROW:PADROW + P, :], padt[:, :]).then_inc(padded, 16)
            sp.wait_ge(s["table"], 1)
            for e in range(E):
                r = sp.value_load(pad_row[0:1, e:e + 1], min_val=0, max_val=PADROW - P)
                sp.dma_start(rows[bass.ds(r, P), :], padt[:, :]).then_inc(padded, 16)
            sp.wait_ge(padded, 16 * (E + 1))
            for i in range(4):
                sp.wait_ge(scattered[i], 16 * NT * (NU // 4))

            def load(turn, k):
                after(sp, stored[k], 16 * turn)
                r = sp.value_load(blk_row[0:1, bass.ds(turn * UN + k, 1)], min_val=0, max_val=PADROW)
                sp.dma_start(XR[k][:, :], rows[bass.ds(r, P), :]).then_inc(row_loaded[k], 16)

            steps(sp, [(0, load)])
            for k in range(UN):
                sp.wait_ge(stored[k], 16 * (NB // UN + (k < NB % UN)))

        @block.gpsimd
        def _(pool):
            pool.memset(bias[:, :], 0.0)
            pool.memset(carry[:, :], 0.0)
            pool.memset(carry16[:, :], 0.0)
            pool.memset(padt[:, :], 0.0)
            pool.memset(mx[:, :], 0.0)
            pool.memset(epsc[:, :], LN_EPS)
            pool.memset(half12[:, :], -0.5)
            for i in range(2):
                pool.memset(pin[i][:, :], 1.0)
            for i in range(4):
                pool.memset(R[i][:, :, D + 3:D + 4], 0.0)
            pool.memset(ones[:, :], 1.0)
            pool.memset(ones16[:, :], 1.0)
            pool.memset(gdz[:, D:D + 1], 1.0).then_inc(s["zeroed"], 1)
            pool.wait_ge(s["zeroed"], 1)
            pool.memset(padt[:, D + 2:D + 3].bitcast(I32), T).then_inc(s["pads_ready"], 1)

            def roots(i):
                pool.wait_ge(s["moments_in"], i + 2)
                pool.tensor_scalar(pgd[:, :], pin[i % 2][:, :], 1e-36, None, ALU.max).then_inc(s["guarded"], 1)
                pool.wait_ge(s["guarded"], i + 2)
                pool.tensor_tensor(prt[i % 2][:, :], pgd[:, :], half12[:, :], ALU.pow).then_inc(s["roots"], 1)

            def scatter(u):
                pool.wait_ge(s["placed"], u + 1)
                pool.wait_ge(s["x1"], u + 1)
                for k in range(NT):
                    pool.indirect_dma_start(
                        out=rows[:, :], out_offset=bass.IndirectOffsetOnAxis(ap=place[u % 4][:, k:k + 1], axis=0),
                        in_=R[u % 4][:, k, :], in_offset=None).then_inc(scattered[u % 4], 16)

            for i in range(-1, NU + 2):
                if i < NU + 1:
                    roots(i)
                if i >= 2:
                    scatter(i - 2)

            def scaled(turn, k):
                pool.wait_ge(row_loaded[k], 16 * (turn + 1))
                pool.nop().then_inc(seen, 1)
                pool.tensor_scalar(cg[k][:, :], XR[k][:, D:D + 1], scl[:, 3:4], None, ALU.mult)
                pool.tensor_scalar(xs[k][:, :], XR[k][:, 0:D], XR[k][:, D + 1:D + 2], None, ALU.mult).then_inc(t["b_xs"], 1)

            def store(turn, k):
                pool.wait_ge(t["b_out"], turn * UN + k + 1)
                pool.nop().then_inc(seen, 1)
                pool.indirect_dma_start(
                    out=out[:, :], out_offset=bass.IndirectOffsetOnAxis(ap=XR[k][:, D + 2:D + 3].bitcast(I32), axis=0),
                    in_=OUT[k][:, :], in_offset=None, bounds_check=T - 1, oob_is_err=False).then_inc(stored[k], 16)

            steps(pool, [(3, scaled), (-1, store)])

        @block.tensor
        def _(pe):
            pe.wait_ge(s["guided"], 1)
            pe.wait_ge(ld["cst"], 16)
            pe.transpose(log_ps[:, 128:128 + G], gdn[:, :], ident[0:G, 0:G]).then_inc(s["guideT_ps"], 1)

            def infl(u):
                pe.wait_ge(s["ET"], u + 1)
                if u >= 1:
                    pe.wait_ge(s["V"], u)
                for k in range(NT):
                    m = pe.matmul(half(infl_ps, k), ET[u % 2][:, k * P:(k + 1) * P], gdz[:, :], start=True, stop=True)
                m.then_inc(s["infl_ps"], 1)

            def xT_(u):
                pe.wait_ge(s["x1"], u + 1)
                if u >= 1:
                    pe.wait_ge(s["xT_sb"], u)
                for k in range(NT):
                    m = pe.transpose(xT_ps[:, k * P:(k + 1) * P], R[u % 4][:, k, 0:D], ident)
                m.then_inc(s["xT_ps"], 1)

            def nT_(u):
                pe.wait_ge(s["n"], u + 1)
                if u >= 1:
                    pe.wait_ge(s["nT_sb"], u)
                for k in range(NT):
                    m = pe.transpose(nT_ps[:, k * P:(k + 1) * P], N[u % 2][:, k, :], ident)
                m.then_inc(s["nT_ps"], 1)

            def traj(u):
                pe.wait_ge(s["V"], u + 1)
                if u >= 1:
                    pe.wait_ge(s["y"], u)
                for k in range(NT):
                    for a in range(2):
                        m = pe.matmul(half(traj_ps, k), band[a][k % 2], V[u % 3][:, 2 * (k // 2) + a, :],
                                      start=a == 0, stop=a == 1)
                m.then_inc(s["traj_ps"], 1)

            def logits(u):
                pe.wait_ge(s["xT_sb"], u + 1)
                if u == 0:
                    pe.wait_ge(s["guideT"], 1)
                    pe.wait_ge(ld["small"], 64)
                if u >= 1:
                    pe.wait_ge(s["placed"], u)
                if u == 3:
                    pe.wait_ge(s["scales_w"], 1)
                for k in range(NT):
                    m = pe.matmul(log_ps[:, k * E:(k + 1) * E], xT[:, k * P:(k + 1) * P], Wr[:, :], start=True, stop=True)
                m.then_inc(s["logits_ps"], 1)

            def sims(u):
                pe.wait_ge(s["nT_sb"], u + 1)
                if u == 0:
                    pe.wait_ge(s["guideT"], 1)
                if u >= 1:
                    pe.wait_ge(s["ET"], u)
                pe.matmul(sims_ps[0:G, :], gdT[:, :], nT[:, :], start=True, stop=True).then_inc(s["sims_ps"], 1)

            def rank(u):
                pe.wait_ge(s["onehot"], u + 1)
                pe.matmul(rank_ps, lt16[:, :], oh16[:, :, :], start=True, stop=False)
                pe.matmul(rank_ps, ones16[:, :], carry16[:, :].unsqueeze(1).to_broadcast([P, NT, E]), start=False, stop=False)
                for k in range(1, NT):
                    m = pe.matmul(rank_ps[:, k * E:], ones16[:, :], oh16[:, 0:NT - k, :], start=False, stop=k == NT - 1)
                m.then_inc(s["rank_ps"], 1)

            for i in range(0, NU + 2):
                if 1 <= i <= NU:
                    infl(i - 1)
                if i >= 2:
                    xT_(i - 2)
                if i < NU:
                    nT_(i)
                if 1 <= i <= NU:
                    traj(i - 1)
                if i >= 2:
                    logits(i - 2)
                if i < NU:
                    sims(i)
                if i >= 2:
                    rank(i - 2)
                if i == 4:
                    pe.wait_ge(s["maxima"], 1)
                    pe.wait_ge(s["placed"], 3)
                    pe.transpose(log_ps[0:4, 128:128 + P], mx[:, 0:4], ident).then_inc(s["maxT_ps"], 1)
                    pe.wait_ge(s["max4"], 1)
                    pe.matmul(log_ps[:, 256:260], ones[0:4, :], mx4[:, 0:4], start=True, stop=True).then_inc(s["maxb_ps"], 1)
            pe.wait_ge(s["counted"], NU)
            pe.matmul(log_ps[:, 300:300 + E], ones16[:, :], carry16[:, :], start=True, stop=True).then_inc(s["tot_ps"], 1)

            pe.wait_ge(s["table"], 1)

            def b_xT(turn, k):
                pe.wait_ge(t["b_xs"], turn * UN + k + 1)
                after(pe, t["b_xh"], turn * UN + k)
                pe.transpose(bank[0][:, 0:P], xs[k][:, :], ident).then_inc(t["b_xT_ps"], 1)

            def b_h(turn, k):
                b = turn * UN + k
                e = pe.value_load(blk_e[0:1, bass.ds(b, 1)], min_val=0, max_val=E - 1)
                pe.wait_ge(t["b_xl"], b + 1)
                after(pe, t["b_hl"], b - 2)
                for c in range(FC):
                    h = bank[1 + k % 3][:, c * P:(c + 1) * P]
                    pe.matmul(h, bias3[:, c * P:(c + 1) * P], sel16[:, bass.ds(b, 1)].to_broadcast([96, P]), start=True, stop=False)
                    wh, wl = W1h[:, bass.ds(e * FF + c * P, P)], W1l[:, bass.ds(e * FF + c * P, P)]
                    pe.matmul(h, wh, xh[k][:, :], start=False, stop=False)
                    pe.matmul(h, wh, xl[k][:, :], start=False, stop=False)
                    m = pe.matmul(h, wl, xh[k][:, :], start=False, stop=True)
                m.then_inc(t["b_h_ps"], 1)

            def b_y(turn, k):
                b = turn * UN + k
                e = pe.value_load(blk_e[0:1, bass.ds(b, 1)], min_val=0, max_val=E - 1)
                y = bank[4 + k % 3]
                pe.wait_ge(t["b_hl"], b + 1)
                after(pe, t["b_z"], b - 2)
                for c in range(FC):
                    pe.matmul(y[:, 0:2 * D], hh[k][:, c * P:(c + 1) * P], W2hl[:, bass.ds(e * FC + c, 1), :], start=c == 0, stop=False)
                    if c == 0:
                        pe.matmul(y[:, 0:D], sel16[:, bass.ds(b, 1)].to_broadcast([96, P]), bias3[:, FF:FF + D], start=False, stop=False)
                    m = pe.matmul(y[:, 0:D], hl[k][:, c * P:(c + 1) * P], W2hl[:, bass.ds(e * FC + c, 1), 0:D], start=False, stop=c == FC - 1)
                m.then_inc(t["b_y_ps"], 1)

            steps(pe, [(2, b_xT), (1, b_h), (0, b_y)])

        @block.scalar
        def _(act):
            act.dma_start(gd[:, :], guide).then_inc(ld["guide"], 16)
            act.dma_start(Wr[:, :], wr).then_inc(ld["small"], 16)
            act.dma_start(brb[:, :], br.rearrange("(a e) -> a e", a=1).to_broadcast([P, E])).then_inc(ld["small"], 16)
            act.dma_start(gb[:, 0:1], ln_g.rearrange("(d a) -> d a", a=1)).then_inc(ld["small"], 16)
            act.dma_start(gb[:, 1:2], ln_b.rearrange("(d a) -> d a", a=1)).then_inc(ld["small"], 16)
            act.wait_ge(s["guide_sq"], 1)
            act.activation(gst[:, 1:2], gst[:, 0:1], ACT.Sqrt).then_inc(s["guide_norm"], 1)
            act.wait_ge(s["zeroed"], 1)
            for q in range(3):
                act.dma_start(bias[32 * q:32 * q + E, 0:FF], b1).then_inc(ld["bias"], 16)
                act.dma_start(bias[32 * q:32 * q + E, FF:FF + D], b2).then_inc(ld["bias"], 16)

            def sumsq(u):
                act.wait_ge(s["diff"], u + 1)
                for k in range(NT):
                    a = act.activation(sq[:, :], Dd[u % 2][:, k // 2, k % 2, :], ACT.Square, accum_out=pin[(u - 1) % 2][:, k:k + 1])
                    act.drain()
                act.nop().then_inc(s["sumsq"], 1)

            def tanh(u):
                act.wait_ge(s["mags"], u + 1)
                act.activation(st[u % 3][:, MT, :], st[u % 3][:, MAG, :], ACT.Tanh, scale=2.0).then_inc(s["tanh"], 1)

            def np_(u):
                act.wait_ge(s["scales"], u + 1)
                if u >= 3:
                    act.wait_ge(s["traj_ps"], u - 2)
                for k in range(NT):
                    act.activation(V[u % 3][:, k, 0:D], Dd[u % 2][:, k // 2, k % 2, :], ACT.Identity, scale=st[u % 3][:, CN, k:k + 1])
                act.activation(V[u % 3][:, :, D], st[u % 3][:, MT, :], ACT.Identity).then_inc(s["np"], 1)

            def nT_(u):
                act.wait_ge(s["nT_ps"], u + 1)
                if u >= 1:
                    act.wait_ge(s["sims_ps"], u)
                act.activation(nT[:, :], nT_ps[:, :], ACT.Identity).then_inc(s["nT_sb"], 1)

            def et(u):
                act.wait_ge(s["sims_ps"], u + 1)
                if u >= 2:
                    act.wait_ge(s["infl_ps"], u - 1)
                act.activation(ET[u % 2][:, :], sims_ps[0:G, :], ACT.Exp, scale=2.0).then_inc(s["ET"], 1)

            def x1(u):
                act.wait_ge(s["x1c"], u + 1)
                for k in range(NT):
                    a = act.activation(R[u % 4][:, k, 0:D], Y[:, k, :], ACT.Identity,
                                       scale=st[u % 3][:, R1, k:k + 1], bias=st[u % 3][:, WR, k:k + 1])
                a.then_inc(s["x1"], 1)

            def xT_(u):
                act.wait_ge(s["xT_ps"], u + 1)
                if u >= 1:
                    act.wait_ge(s["logits_ps"], u)
                act.activation(xT[:, :], xT_ps[:, :], ACT.Identity).then_inc(s["xT_sb"], 1)

            def rexp(u):
                act.wait_ge(s["shifted"], u + 1)
                act.activation(ex[:, :, :], lg[:, :, :], ACT.Exp).then_inc(s["exped"], 1)

            def weights_hi():
                act.wait_ge(s["scales_w"], 1)
                for e in range(0, E, 2):
                    act.activation(W1h[:, e * FF:(e + 2) * FF], W1[:, e:e + 2, :], ACT.Identity, scale=scl[:, 1:2])
                    act.activation(W2hl[:, e * FC:(e + 2) * FC, 0:D], W2[:, e:e + 2, :, :], ACT.Identity,
                                   scale=scl[:, 2:3]).then_inc(s["split_hi"], 1)

            for i in range(-1, NU + 2):
                if 2 <= i:
                    xT_(i - 2)
                if 0 <= i < NU:
                    nT_(i)
                if i + 1 < NU:
                    sumsq(i + 1)
                if 0 <= i < NU:
                    et(i)
                if 2 <= i:
                    rexp(i - 2)
                if i + 1 < NU:
                    tanh(i + 1)
                    np_(i + 1)
                if 1 <= i <= NU:
                    x1(i - 1)
                if i == 4:
                    weights_hi()

            act.wait_ge(s["table"], 1)

            def b_xt(turn, k):
                act.wait_ge(t["b_xT_ps"], turn * UN + k + 1)
                act.activation(xt[k][:, :], bank[0][:, 0:P], ACT.Identity, scale=gbs[:, 0:1], bias=gbs[:, 1:2])
                act.activation(xh[k][:, :], bank[0][:, 0:P], ACT.Identity, scale=gbs[:, 0:1], bias=gbs[:, 1:2]).then_inc(t["b_xh"], 1)

            def b_hh(turn, k):
                act.wait_ge(t["b_h_ps"], turn * UN + k + 1)
                act.activation(hh[k][:, :], bank[1 + k % 3][:, :], ACT.Relu).then_inc(t["b_hh"], 1)

            def b_sd(turn, k):
                act.wait_ge(t["b_mv"], turn * UN + k + 1)
                act.activation(sd[k][:, 0:1], mv2[k][:, 1:2], ACT.Sqrt, bias=epsc[:, 0:1]).then_inc(t["b_sd"], 1)

            steps(act, [(2, b_xt), (1, b_hh), (-1, b_sd)])

        @block.vector
        def _(dve):
            tt, ts, stt = dve.tensor_tensor, dve.tensor_scalar, dve.scalar_tensor_tensor

            dve.wait_ge(ld["guide"], 16)
            dve.wait_ge(s["zeroed"], 1)
            tt(gdn[:, :], gd[:, :], gd[:, :], ALU.mult)
            ts(gdz[:, 0:D], gd[:, :], GUIDE, None, ALU.mult)
            dve.drain()
            dve.tensor_reduce(gst[:, 0:1], gdn[:, :], AX.X, ALU.add).then_inc(s["guide_sq"], 1)
            dve.wait_ge(s["guide_norm"], 1)
            ts(gst[:, 2:3], gst[:, 1:2], EPS_COS, None, ALU.max)
            dve.drain()
            dve.reciprocal(gst[:, 3:4], gst[:, 2:3])
            dve.drain()
            ts(gdn[:, :], gd[:, :], gst[:, 3:4], None, ALU.mult).then_inc(s["guided"], 1)
            dve.wait_ge(s["guideT_ps"], 1)
            dve.tensor_copy(gdT[:, :], log_ps[:, 128:128 + G]).then_inc(s["guideT"], 1)
            dve.wait_ge(ld["cst"], 16)
            dve.tensor_copy(lt16[:, :], C[:, C_LT:C_LT + P])

            def diff(u):
                g = [0, 1, 1, 2, 2, 3, 3, 3][u]
                dve.wait_ge(ld[f"x{g}"], 32 if g < 3 else 64)
                if u >= 2:
                    dve.wait_ge(s["np"], u - 1)
                b = slice(2 * u, 2 * u + 2)
                tt(Dd[u % 2][:, :, 0, :], X[:, b, 1, :], X[:, b, 0, :], ALU.subtract)
                tt(Dd[u % 2][:, :, 1, :], XN[:, b, :], X[:, b, 1, :], ALU.subtract).then_inc(s["diff"], 1)

            def blend(u):
                q, zi = st[u % 3][:, Q, :], st[u % 3][:, ZI, :]
                dve.wait_ge(s["infl_ps"], u + 1)
                for h in range(2):
                    dve.reciprocal(zi[:, 2 * h:2 * h + 2].unsqueeze(2), pair(infl_ps[h])[:, :, D:D + 1])
                dve.drain()
                tt(q, zi, st[u % 3][:, MT, :], ALU.mult)
                dve.drain()
                dve.wait_ge(s["np"], u + 1)
                for k in range(NT):
                    a = stt(V[u % 3][:, k, 0:D], half(infl_ps, k)[:, 0:D], q[:, k:k + 1], V[u % 3][:, k, 0:D], ALU.mult, ALU.add)
                a.then_inc(s["V"], 1)

            def norm1(u):
                wi = st[u % 3][:, WI, :]
                dve.wait_ge(s["traj_ps"], u + 1)
                for h in range(2):
                    ts(wi[:, 2 * h:2 * h + 2].unsqueeze(2), pair(traj_ps[h])[:, :, D:D + 1], EPS_WSUM, None, ALU.max)
                dve.drain()
                dve.reciprocal(st[u % 3][:, SS, :], wi)
                dve.drain()
                if u >= 1:
                    dve.wait_ge(s["x1"], u)
                for k in range(NT):
                    a = stt(Y[:, k, :], half(traj_ps, k)[:, 0:D], st[u % 3][:, SS, k:k + 1], X[:, 2 * u + k // 2, k % 2, :],
                            ALU.mult, ALU.add)
                a.then_inc(s["y"], 1)
                dve.drain()
                for k in range(NT):
                    dve.bn_stats(bn[:, k, :], Y[:, k, :])
                dve.drain()
                for k in range(NT):
                    dve.bn_aggr(mv[u % 2][:, k, :], bn[:, k, :])
                dve.drain()
                vp = pin[(u + 1) % 2]
                ts(vp[:, 4:8], mv[u % 2][:, :, 1], LN_EPS, None, ALU.add)
                dve.drain()
                dve.reciprocal(st[u % 3][:, WI, :], vp[:, 4:8])
                dve.drain()
                tt(st[u % 3][:, VP, :], mv[u % 2][:, :, 1], st[u % 3][:, WI, :], ALU.mult)
                dve.drain()
                ts(vp[:, 8:12], st[u % 3][:, VP, :], LN_EPS, None, ALU.add)

            def moments(i):
                if i + 1 < NU:
                    dve.wait_ge(s["sumsq"], i + 2)
                dve.drain().then_inc(s["moments_in"], 1)

            def router(u):
                dve.wait_ge(s["logits_ps"], u + 1)
                if u == 0:
                    dve.wait_ge(ld["small"], 64)
                tt(lg[:, :, :], log_ps[:, 0:NT * E].rearrange("p (k e) -> p k e", k=NT), brb[:, :].unsqueeze(1).to_broadcast([P, NT, E]), ALU.add)
                dve.drain()
                dve.tensor_reduce(rt[:, 0, :], lg[:, :, :], AX.X, ALU.max)
                dve.drain()
                tt(lg[:, :, :], lg[:, :, :], rt[:, 0, :].unsqueeze(2).to_broadcast([P, NT, E]), ALU.subtract).then_inc(s["shifted"], 1)
                dve.drain()
                stt(oh[:, :, :], lg[:, :, :], 0.0, C[:, C_REV:C_REV + E].unsqueeze(1).to_broadcast([P, NT, E]), ALU.is_ge, ALU.mult)
                dve.drain()
                dve.tensor_reduce(rt[:, 1, :], oh[:, :, :], AX.X, ALU.max)
                dve.drain()
                tt(oh[:, :, :], oh[:, :, :], rt[:, 1, :].unsqueeze(2).to_broadcast([P, NT, E]), ALU.is_equal)
                dve.drain()
                dve.tensor_copy(oh16[:, :, :], oh[:, :, :]).then_inc(s["onehot"], 1)

            def placing(u):
                dve.wait_ge(s["rank_ps"], u + 1)
                if u >= 4:
                    dve.wait_ge(scattered[u % 4], 16 * NT * (u // 4))
                tt(pl[:, :, :], rank_ps.rearrange("p (k e) -> p k e", k=NT), C[:, C_REG:C_REG + E].unsqueeze(1).to_broadcast([P, NT, E]), ALU.add)
                dve.tensor_reduce(cnt[:, :], oh[:, :, :].rearrange("p k e -> p e k"), AX.X, ALU.add)
                dve.wait_ge(s["exped"], u + 1)
                dve.tensor_reduce(rt[:, 2, :], ex[:, :, :], AX.X, ALU.add)
                dve.drain()
                dve.reciprocal(R[u % 4][:, :, D], rt[:, 2, :])
                tt(pl[:, :, :], pl[:, :, :], oh[:, :, :], ALU.mult)
                tt(carry[:, :], carry[:, :], cnt[:, :], ALU.add)
                dve.drain()
                dve.tensor_reduce(rt[:, 3, :], pl[:, :, :], AX.X, ALU.add)
                dve.drain()
                dve.tensor_copy(place[u % 4][:, :], rt[:, 3, :]).then_inc(s["placed"], 1)
                dve.tensor_copy(carry16[:, :], carry[:, :]).then_inc(s["counted"], 1)

            def mags(u):
                m = st[u % 3]
                r = prt[(u - 1) % 2]
                dve.wait_ge(s["roots"], u + 1)
                tt(m[:, MAG, :], pin[(u - 1) % 2][:, 0:NT], r[:, 0:NT], ALU.mult)
                dve.drain()
                stt(m[:, INV, :], m[:, MAG, :], EPS_MAG, r[:, 0:NT], ALU.is_gt, ALU.mult).then_inc(s["mags"], 1)
                dve.drain()
                if u >= 2:
                    dve.wait_ge(s["nT_ps"], u - 1)
                for k in range(NT):
                    a = ts(N[u % 2][:, k, :], Dd[u % 2][:, k // 2, k % 2, :], m[:, INV, k:k + 1], None, ALU.mult)
                a.then_inc(s["n"], 1)
                dve.wait_ge(s["tanh"], u + 1)
                stt(m[:, CN, :], m[:, MT, :], 1.0 - GUIDE, m[:, INV, :], ALU.mult, ALU.mult).then_inc(s["scales"], 1)

            def center(u):
                r = prt[(u + 1) % 2]
                dve.wait_ge(s["roots"], u + 3)
                if u >= 4:
                    dve.wait_ge(scattered[u % 4], 16 * NT * (u // 4))
                stt(st[u % 3][:, WR, :], mv[u % 2][:, :, 0], -1.0, r[:, 4:8], ALU.mult, ALU.mult)
                dve.tensor_copy(st[u % 3][:, R1, :], r[:, 4:8])
                dve.tensor_copy(R[u % 4][:, :, D + 1], r[:, 8:12])
                dve.tensor_copy(R[u % 4][:, :, D + 2].bitcast(I32), C[:, C_TOK + u * NT:C_TOK + (u + 1) * NT]).then_inc(s["x1c"], 1)

            def maxima(q):
                if q == 0:
                    dve.wait_ge(ld["w1"], 16)
                    dve.wait_ge(ld["w2"], 16)
                dve.tensor_reduce(mx[:, 4 + q:5 + q], W1[:, 2 * q:2 * q + 2, :], AX.XY, ALU.max, apply_absolute_value=True)
                dve.tensor_reduce(mx[:, 8 + q:9 + q], W2[:, 2 * q:2 * q + 2, :, :], AX.XYZ, ALU.max, apply_absolute_value=True)
                if q == 3:
                    dve.wait_ge(ld["bias"], 96)
                    dve.drain()
                    stt(mx[:, 12:14], gb[:, :], -1.0, gb[:, :], ALU.mult, ALU.max)
                    dve.tensor_reduce(mx[:, 1:2], mx[:, 4:8], AX.X, ALU.max)
                    dve.tensor_reduce(mx[:, 2:3], mx[:, 8:12], AX.X, ALU.max)
                    dve.tensor_reduce(mx[0:96, 3:4], bias[:, 0:FF], AX.X, ALU.max, apply_absolute_value=True)
                    dve.drain()
                    stt(mx[:, 0:1], mx[:, 12:13], 11.5, mx[:, 13:14], ALU.mult, ALU.add).then_inc(s["maxima"], 1)

            def scales():
                dve.wait_ge(s["maxT_ps"], 1)
                dve.tensor_reduce(mx4[:, 4:5], log_ps[0:4, 128:128 + P], AX.X, ALU.max)
                dve.drain()
                ts(mx4[:, 0:4], ident[0:4, 0:4], mx4[:, 4:5], None, ALU.mult).then_inc(s["max4"], 1)
                dve.wait_ge(s["maxb_ps"], 1)
                LO = 2.0 ** -40
                v = scl[:, 8:12]
                ts(v, log_ps[:, 256:260], LO, None, ALU.max)
                dve.drain()

                def power(dst, src, k):
                    ts(dst.bitcast(I32), src.bitcast(I32), POW2_MASK, None, ALU.bitwise_and)
                    dve.drain()
                    ts(dst.bitcast(I32), dst.bitcast(I32), -1.0, float((254 + k) << 23), ALU.mult, ALU.add)
                    dve.drain()

                power(scl[:, 0:1], v[:, 0:1], 5)
                power(scl[:, 2:3], v[:, 2:3], 8)
                tt(scl[:, 12:13], v[:, 3:4], scl[:, 0:1], ALU.mult)
                ts(scl[:, 13:14], v[:, 1:2], 0.5, None, ALU.mult)
                dve.drain()
                stt(scl[:, 14:15], scl[:, 12:13], 2.0 ** -13, scl[:, 13:14], ALU.mult, ALU.max)
                dve.drain()
                power(scl[:, 1:2], scl[:, 14:15], 0)
                tt(scl[:, 4:5], scl[:, 0:1], scl[:, 1:2], ALU.mult)
                dve.drain()
                tt(scl[:, 5:6], scl[:, 4:5], scl[:, 2:3], ALU.mult)
                ts(gbs[:, :], gb[:, :], scl[:, 0:1], None, ALU.mult)
                dve.drain()
                power(scl[:, 3:4], scl[:, 5:6], 0)
                ts(bias[:, 0:FF], bias[:, 0:FF], scl[0:96, 4:5], None, ALU.mult)
                ts(bias[:, FF:FF + D], bias[:, FF:FF + D], scl[0:96, 5:6], None, ALU.mult).then_inc(s["scales_w"], 1)

            def split_bias():
                dve.tensor_copy(bias_h[:, :], bias[:, :])
                dve.drain()
                tt(bias_r[:, :], bias[:, :], bias_h[:, :], ALU.subtract)
                dve.drain()
                dve.tensor_copy(bias_m[:, :], bias_r[:, :])
                dve.drain()
                tt(bias_l[:, :], bias_r[:, :], bias_m[:, :], ALU.subtract)
                dve.tensor_copy(bias3[0:32, :], bias_h[0:32, :])
                dve.tensor_copy(bias3[32:64, :], bias_m[32:64, :])
                dve.drain()
                dve.tensor_copy(bias3[64:96, :], bias_l[64:96, :])

            def split_lo(q):
                dve.wait_ge(s["split_hi"], q + 1)
                e2 = slice(2 * q * FF, (2 * q + 2) * FF)
                stt(W1l[:, e2].rearrange("p (e f) -> p e f", e=2), W1[:, 2 * q:2 * q + 2, :], scl[:, 1:2],
                    W1h[:, e2].rearrange("p (e f) -> p e f", e=2), ALU.mult, ALU.subtract)
                w = W2hl[:, 2 * q * FC:(2 * q + 2) * FC, :]
                stt(w[:, :, D:2 * D], W2[:, 2 * q:2 * q + 2, :, :].rearrange("p e c d -> p (e c) d"), scl[:, 2:3], w[:, :, 0:D], ALU.mult, ALU.subtract)

            diff(0)
            for i in range(-1, NU + 2):
                if 0 <= i and i + 1 < NU:
                    diff(i + 1)
                if 1 <= i <= NU:
                    blend(i - 1)
                    norm1(i - 1)
                if i <= NU:
                    moments(i)
                if 0 <= i < 4:
                    maxima(i)
                if i == 5:
                    split_bias()
                if 5 <= i < 9:
                    split_lo(i - 5)
                if i >= 2:
                    router(i - 2)
                if i + 1 < NU:
                    mags(i + 1)
                if 1 <= i <= NU:
                    center(i - 1)
                if i >= 2:
                    placing(i - 2)
                if i == 4:
                    scales()

            dve.wait_ge(s["tot_ps"], 1)
            dve.tensor_copy(tot[:, :], log_ps[:, 300:300 + E])
            dve.drain()
            ts(nblk_i[:, :], tot[:, :], float(P - 1), None, ALU.add)
            tt(pad_row[:, :], tot[:, :], C[:, C_REG:C_REG + E], ALU.add)
            dve.drain()
            ts(nblk_i[:, :], nblk_i[:, :], 7, None, ALU.arith_shift_right)
            dve.drain()
            dve.tensor_copy(nblk[:, :], nblk_i[:, :])
            dve.drain()
            dve.tensor_tensor_scan(cend[:, :], ones[:, 0:E], nblk[:, :], 0.0, ALU.mult, ALU.add)
            ts(jump[:, :], nblk[:, :], -float(P), float(REG), ALU.mult, ALU.add)
            dve.drain()
            tt(past[:, :, :], cend[:, :].unsqueeze(1).to_broadcast([P, NB, E]),
               C[:, C_BLK:C_BLK + NB].unsqueeze(2).to_broadcast([P, NB, E]), ALU.is_le)
            dve.drain()
            dve.tensor_reduce(blk[:, 0, :], past[:, :, :], AX.X, ALU.add)
            tt(past2[:, :, :], past[:, :, :], jump[:, :].unsqueeze(1).to_broadcast([P, NB, E]), ALU.mult)
            dve.drain()
            dve.tensor_reduce(blk[:, 1, :], past2[:, :, :], AX.X, ALU.add)
            ts(blk[:, 0, :], blk[:, 0, :], float(E - 1), None, ALU.min)
            dve.drain()
            stt(blk[:, 2, :], C[:, C_BLK:C_BLK + NB], float(P), blk[:, 1, :], ALU.mult, ALU.add)
            dve.tensor_copy(blk_e[:, :], blk[:, 0, :])
            ts(sel16[:, :], blk[0:96, 0, :], C[0:96, C_EID:C_EID + 1], None, ALU.is_equal)
            dve.drain()
            ts(blk_row[:, :], blk[:, 2, :], float(PADROW), None, ALU.min)
            dve.drain().then_inc(s["table"], 1)

            def b_xl(turn, k):
                dve.wait_ge(t["b_xh"], turn * UN + k + 1)
                tt(xl[k][:, :], xt[k][:, :], xh[k][:, :], ALU.subtract).then_inc(t["b_xl"], 1)

            def b_hl(turn, k):
                dve.wait_ge(t["b_hh"], turn * UN + k + 1)
                stt(hl[k][:, :], bank[1 + k % 3][:, :], 0.0, hh[k][:, :], ALU.max, ALU.subtract).then_inc(t["b_hl"], 1)

            def b_fin(turn, k):
                dve.wait_ge(t["b_sd"], turn * UN + k + 1)
                dve.reciprocal(sd[k][:, 1:2], sd[k][:, 0:1])
                dve.drain()
                ts(OUT[k][:, :], z[k][:, :], mv2[k][:, 0:1], sd[k][:, 1:2], ALU.subtract, ALU.mult).then_inc(t["b_out"], 1)

            def b_z(turn, k):
                y = bank[4 + k % 3]
                dve.wait_ge(t["b_xs"], turn * UN + k + 1)
                dve.wait_ge(t["b_y_ps"], turn * UN + k + 1)
                stt(z0[:, :], y[:, 0:D], cg[k][:, :], XR[k][:, 0:D], ALU.mult, ALU.add)
                dve.drain()
                stt(z[k][:, :], y[:, D:2 * D], cg[k][:, :], z0[:, :], ALU.mult, ALU.add).then_inc(t["b_z"], 1)
                dve.drain()
                dve.bn_stats(bn2[:, :], z[k][:, :])
                dve.drain()
                dve.bn_aggr(mv2[k][:, :], bn2[:, :]).then_inc(t["b_mv"], 1)

            steps(dve, [(2, b_xl), (1, b_hl), (-1, b_fin), (0, b_z)])


def kernel(**inputs):
    import concourse.bacc as bacc
    from concourse.bass_utils import run_bass_kernel_spmd

    nc = bacc.Bacc("TRN2", target_bir_lowering=False, num_devices=1)
    arrays, aps = {}, []
    names = ("attn_embeddings", "attn_guidance_trajectories", "ffn_Wr", "ffn_br", "ffn_ln_g", "ffn_ln_b",
             "ffn_W1", "ffn_b1", "ffn_W2", "ffn_b2")
    for name in names:
        a = np.ascontiguousarray(inputs["L0_" + name])
        arrays["in_" + name] = a
        aps.append(nc.dram_tensor("in_" + name, a.shape, mybir.dt.from_np(a.dtype), kind="ExternalInput").ap())
    arrays["in_constants"] = constants()
    aps.append(nc.dram_tensor("in_constants", (P, C_N), F32, kind="ExternalInput").ap())
    rows = nc.dram_tensor("rows", (PADROW + P, ROW), F32, kind="Internal").ap()
    out = nc.dram_tensor("out", (T, D), F32, kind="ExternalOutput").ap()
    build(nc, *aps, rows, out)
    r = run_bass_kernel_spmd(nc, [arrays], core_ids=[0])
    return r.results[0]["out"].reshape(B, S, D)
```

```python
from contextlib import ExitStack

import numpy as np

import concourse.bass as bass
from concourse import mybir

F32 = mybir.dt.float32
F16 = mybir.dt.float16
BF16 = mybir.dt.bfloat16
I32 = mybir.dt.int32
ALU = mybir.AluOpType
ACT = mybir.ActivationFunctionType
AX = mybir.AxisListType

P = 128
B, S, D = 16, 256, 128
T = B * S
E, FF = 8, 512
FC = FF // P
G = 64
W = 8
NT = 4
NU = T // (NT * P)
REG = T + P
PADROW = E * REG
NB = (T + E * (P - 1)) // P
ROW = D + 4
UN = 8
LN_EPS = 1e-5
EPS_MAG, EPS_COS, EPS_WSUM, GUIDE = 1e-6, 1e-8, 1e-8, 0.4
POW2_MASK = 0x7F800000

C_BAND = 0
C_ID = C_BAND + 4 * P
C_LT = C_ID + P
C_REG = C_LT + P
C_REV = C_REG + E
C_BLK = C_REV + E
C_TOK = C_BLK + NB
C_EID = C_TOK + NU * NT
C_N = C_EID + 1


def constants():
    c = np.zeros((P, C_N), np.float32)
    for s in range(1, S):
        w = min(s, W)
        for j in range(w):
            i = s - w + j
            v = np.float32(0.1) + np.float32(0.9) * np.float32(j) / np.float32(max(w - 1, 1)) if w > 1 else 0.1
            c[i // 2, C_BAND + (2 * (i % 2) + s % 2) * P + s // 2] = v
    c[:, C_ID:C_ID + P] = np.eye(P)
    c[:, C_LT:C_LT + P] = np.triu(np.ones((P, P)), 1)
    c[:, C_REG:C_REG + E] = np.arange(E) * REG
    c[:, C_REV:C_REV + E] = E - np.arange(E)
    c[:, C_BLK:C_BLK + NB] = np.arange(NB)
    p = np.arange(P)
    for u in range(NU):
        for k in range(NT):
            c[:, C_TOK + u * NT + k] = (2 * u + k // 2) * S + 2 * p + k % 2
    c[:, C_EID] = np.where((p % 32 < E) & (p < 96), p % 32, -1)
    return c


def build(nc, x, guide, wr, br, ln_g, ln_b, w1, b1, w2, b2, cst, rows, out):
    with ExitStack() as ctx:
        def sb(name, shape, dt=F32):
            return ctx.enter_context(nc.sbuf_tensor(name, shape, dt))

        def sem(name):
            return ctx.enter_context(nc.semaphore(name))

        bank = [ctx.enter_context(nc.psum_tensor(f"bank{i}", [P, 512], F32)) for i in range(8)]

        C = sb("C", [P, C_N])
        lt16 = sb("lt16", [P, P], BF16)
        ones16 = sb("ones16", [P, P], BF16)
        ones = sb("ones", [P, P])
        gd = sb("gd", [G, D])
        gdn = sb("gdn", [G, D])
        gdT = sb("gdT", [P, G])
        gdz = sb("gdz", [G, D + 1])
        gst = sb("gst", [G, 4])
        epsc = sb("epsc", [P, 1])
        warm = sb("warm", [P, 2])
        Wr = sb("Wr", [P, E])
        brb = sb("brb", [P, E])
        gb = sb("gb", [P, 2])
        gbs = sb("gbs", [P, 2])
        W1 = sb("W1", [P, E, FF])
        W2 = sb("W2", [P, E, FC, D])
        W1h = sb("W1h", [P, E * FF], F16)
        W1l = sb("W1l", [P, E * FF], F16)
        W2hl = sb("W2hl", [P, E * FC, 2 * D], F16)
        bias = sb("bias", [96, FF + D])
        bias_r = sb("bias_r", [96, FF + D])
        bias_h = sb("bias_h", [96, FF + D], BF16)
        bias_m = sb("bias_m", [96, FF + D], BF16)
        bias_l = sb("bias_l", [96, FF + D], BF16)
        bias3 = sb("bias3", [96, FF + D], BF16)
        mx = sb("mx", [P, 16])
        mx4 = sb("mx4", [4, 8])
        scl = sb("scl", [P, 16])

        X = sb("X", [P, B, 2, D])
        XN = sb("XN", [P, B, D])
        Dd = [sb(f"Dd{i}", [P, 2, 2, D]) for i in range(3)]
        sq = sb("sq", [P, D])
        N = [sb(f"N{i}", [P, NT, D]) for i in range(2)]
        V = [sb(f"V{i}", [P, NT, D + 1]) for i in range(3)]
        nT = sb("nT", [P, NT * P])
        ET = [sb(f"ET{i}", [G, NT * P]) for i in range(2)]
        pin = [sb(f"pin{i}", [P, 12]) for i in range(2)]
        prt = [sb(f"prt{i}", [P, 12]) for i in range(2)]
        pgd = sb("pgd", [P, 12])
        half12 = sb("half12", [P, 12])
        st = [sb(f"st{i}", [P, 12, NT]) for i in range(3)]
        Y = [sb(f"Y{i}", [P, NT, D]) for i in range(2)]
        bn = sb("bn", [P, NT, 6])
        mv = [sb(f"mv{i}", [P, NT, 2]) for i in range(2)]
        R = [sb(f"R{i}", [P, NT, ROW]) for i in range(4)]
        xT = sb("xT", [P, NT * P])
        lg = sb("lg", [P, NT, E])
        ex = sb("ex", [P, NT, E])
        oh = sb("oh", [P, NT, E])
        oh16 = sb("oh16", [P, NT, E], BF16)
        carry = sb("carry", [P, E])
        carry16 = sb("carry16", [P, E], BF16)
        rt = sb("rt", [P, 4, NT])
        place = [sb(f"place{i}", [P, NT], I32) for i in range(4)]

        tot = sb("tot", [P, E])
        nblk = sb("nblk", [P, E])
        nblk_i = sb("nblk_i", [P, E], I32)
        pl = sb("pl", [P, NT, E])
        cnt = sb("cnt", [P, E])
        cend = sb("cend", [P, E])
        jump = sb("jump", [P, E])
        past = sb("past", [P, NB, E])
        past2 = sb("past2", [P, NB, E])
        blk = sb("blk", [P, 3, NB])
        blk_e = sb("blk_e", [P, NB], I32)
        blk_row = sb("blk_row", [P, NB], I32)
        pad_row = sb("pad_row", [P, E], I32)
        sel16 = sb("sel16", [96, NB], BF16)
        padt = sb("padt", [P, ROW])

        XR = [sb(f"XR{i}", [P, ROW]) for i in range(UN)]
        tok = [sb(f"tok{i}", [P, 1], I32) for i in range(UN)]
        xs = [sb(f"xs{i}", [P, D]) for i in range(UN)]
        cg = [sb(f"cg{i}", [P, 1]) for i in range(UN)]
        xt = [sb(f"xt{i}", [P, P]) for i in range(UN)]
        xh = [sb(f"xh{i}", [P, P], F16) for i in range(UN)]
        xl = [sb(f"xl{i}", [P, P], F16) for i in range(UN)]
        hh = [sb(f"hh{i}", [P, FF], F16) for i in range(UN)]
        hl = [sb(f"hl{i}", [P, FF], F16) for i in range(UN)]
        z0 = [sb(f"zpart{i}", [P, D]) for i in range(UN)]
        z = [sb(f"z{i}", [P, D]) for i in range(UN)]
        bn2 = [sb(f"bn2{i}", [P, 6]) for i in range(UN)]
        mv2 = [sb(f"mv2{i}", [P, 2]) for i in range(UN)]
        sd = [sb(f"sd{i}", [P, 2]) for i in range(UN)]
        OUT = [sb(f"OUT{i}", [P, D]) for i in range(UN)]

        ld = {n: sem("ld_" + n) for n in ("cst", "guide", "small", "x0", "x1", "x2", "x3", "w1", "w2", "bias")}
        names = ("zeroed diff sumsq moments_in guarded roots mags tanh scales n np nT_ps nT_sb sims_ps ET "
                 "infl_ps V traj_ps y mvd roots2 x1c x1 xT_ps xT_sb logits_ps shifted exped onehot rank_ps placed "
                 "counted guide_sq guide_norm guided guideT_ps guideT split_hi split_lo maxima maxT_ps max4 maxb_ps scales_w "
                 "bias3 tot_ps pad_rows table pads_ready").split()
        s = {n: sem(n) for n in names}
        scattered = [sem(f"scattered{i}") for i in range(4)]
        padded = sem("padded")
        names2 = "xs xh xl hl z".split()
        t = {n: [sem(f"b_{n}{i}") for i in range(UN)] for n in names2}
        every = {n: sem("every_" + n) for n in "token xT_ps xt h_ps hh y_ps z0 mv sd rec out".split()}
        seen = sem("seen")
        row_loaded = [sem(f"row_loaded{i}") for i in range(UN)]
        stored = [sem(f"stored{i}") for i in range(UN)]

        band = [[C[:, C_BAND + (2 * a + b) * P:C_BAND + (2 * a + b + 1) * P] for b in range(2)] for a in range(2)]
        ident = C[:, C_ID:C_ID + P]
        nT_ps, sims_ps = bank[0], bank[1]
        infl_ps, traj_ps, xT_ps, log_ps = [bank[2], bank[3]], [bank[4], bank[5]], bank[6], bank[7]
        rank_ps = log_ps[:, 64:64 + NT * E]

        def half(banks, k):
            return banks[k // 2][:, (k % 2) * (D + 1):(k % 2 + 1) * (D + 1)]

        def pair(b):
            return b[:, 0:2 * (D + 1)].rearrange("p (k d) -> p k d", k=2)

        block = ctx.enter_context(nc.Block())

        MAG, MAGC, INV, CN, MT, Q, ZI, WI, R1, SS, VP, WR = range(12)

        def after(eng, signal, count):
            if not isinstance(count, int) or count > 0:
                eng.wait_ge(signal, count)

        def steps(eng, stages):
            hi = max(lead for lead, _ in stages)
            lo = min(lead for lead, _ in stages)
            def straight(b0, b1):
                for b in range(b0, b1):
                    for lead, f in stages:
                        if 0 <= b + lead < NB:
                            f(lambda d, turn=(b + lead) // UN: turn + d, (b + lead) % UN)
            turns = (NB - hi) // UN
            straight(-hi, UN)
            with eng.Fori(1, turns) as turn:
                held = {}
                def count(d):
                    if d not in held:
                        held[d] = eng.snap(turn + d) if d else turn
                    return held[d]
                for k in range(UN):
                    for lead, f in stages:
                        f(lambda d, more=(k + lead) // UN: count(d + more), (k + lead) % UN)
            straight(turns * UN, NB - lo)

        def blocks(turn, k):
            return turn * UN + k + 1

        def pads(eng, kind, experts):
            for e in experts:
                r = nc.values_load(pad_row[0:1, e:e + 1], engines=(kind,), min_val=0, max_val=PADROW - P,
                                   skip_runtime_bounds_check_because="an expert's region holds all tokens and a block of padding")
                eng.dma_start(rows[bass.ds(r, P), :], padt[:, :]).then_inc(padded, 16)

        @block.sync
        def _(sp):
            sp.dma_start(X[:, 0:2, :, :], x[0:2].rearrange("b (p c) d -> p b (c d)", c=2).rearrange(
                "p b (c d) -> p b c d", c=2)).then_inc(ld["x0"], 16)
            nxt = x.rearrange("b s d -> (b s) d")
            nv = nxt[2:T, :].rearrange("(n c) d -> n c d", c=2)[:, 0, :]
            def next_rows(b0, b1, which):
                if b1 < B:
                    sp.dma_start(XN[:, b0:b1, :], nv[b0 * P:b1 * P, :].rearrange("(b p) d -> p b d", p=P)).then_inc(ld[which], 16)
                else:
                    sp.dma_start(XN[:, b0:B - 1, :], nv[b0 * P:(B - 1) * P, :].rearrange("(b p) d -> p b d", p=P)).then_inc(ld[which], 16)
                    sp.dma_start(XN[0:P - 1, B - 1, :], nv[(B - 1) * P:B * P - 1, :]).then_inc(ld[which], 16)
                    sp.dma_start(XN[P - 1:P, B - 1, :], nxt[T - 1:T, :]).then_inc(ld[which], 16)
            next_rows(0, 2, "x0")
            sp.dma_start(C[:, :], cst).then_inc(ld["cst"], 16)
            for n, (a, b) in enumerate(((2, 6), (6, 10), (10, 16)), 1):
                sp.dma_start(X[:, a:b, :, :], x[a:b].rearrange("b (p c) d -> p b c d", c=2)).then_inc(ld[f"x{n}"], 16)
                next_rows(a, b, f"x{n}")
            sp.dma_start(W1[:, :, :], w1.rearrange("e d f -> d e f")).then_inc(ld["w1"], 16)
            sp.dma_start(W2[:, :, :, :], w2.rearrange("e (c p) d -> p e c d", p=P)).then_inc(ld["w2"], 16)
            sp.wait_ge(s["zeroed"], 1)
            for j in range(3):
                sp.dma_start(bias[32 * j:32 * j + E, 0:FF], b1).then_inc(ld["bias"], 16)
                sp.dma_start(bias[32 * j:32 * j + E, FF:FF + D], b2).then_inc(ld["bias"], 16)
            sp.wait_ge(s["pads_ready"], 1)
            sp.dma_start(rows[PADROW:PADROW + P, :], padt[:, :]).then_inc(padded, 16)
            sp.wait_ge(s["pad_rows"], 1)
            pads(sp, mybir.EngineType.SP, range(0, E // 2))
            sp.wait_ge(s["table"], 1)
            sp.wait_ge(padded, 16 * (E + 1))
            for i in range(4):
                sp.wait_ge(scattered[i], 16 * NT * (NU // 4))

            def load(count, k):
                after(sp, every["z0"], blocks(count(-1), k))
                after(sp, every["token"], blocks(count(-1), k))
                r = nc.values_load(blk_row[0:1, bass.ds(count(0) * UN + k, 1)], engines=(mybir.EngineType.SP,), min_val=0, max_val=PADROW,
                                   skip_runtime_bounds_check_because="the table is clamped to these bounds")
                sp.dma_start(XR[k][:, :], rows[bass.ds(r, P), :]).then_inc(row_loaded[k], 16)

            steps(sp, [(0, load)])
            for k in range(UN):
                sp.wait_ge(stored[k], 16 * (NB // UN + (k < NB % UN)))

        @block.gpsimd
        def _(pool):
            pool.memset(bias[:, :], 0.0)
            pool.memset(carry[:, :], 0.0)
            pool.memset(carry16[:, :], 0.0)
            pool.memset(padt[:, :], 0.0)
            pool.memset(mx[:, :], 0.0)
            pool.memset(epsc[:, :], LN_EPS)
            pool.memset(half12[:, :], -0.5)
            for i in range(2):
                pool.memset(pin[i][:, :], 1.0)
            for i in range(4):
                pool.memset(R[i][:, :, D + 3:D + 4], 0.0)
            pool.memset(ones[:, :], 1.0)
            pool.memset(ones16[:, :], 1.0)
            pool.memset(gdz[:, D:D + 1], 1.0).then_inc(s["zeroed"], 1)
            pool.wait_ge(s["zeroed"], 1)
            pool.memset(padt[:, D + 2:D + 3].bitcast(I32), T).then_inc(s["pads_ready"], 1)

            def roots(i):
                pool.wait_ge(s["moments_in"], i + 2)
                pool.tensor_scalar(pgd[:, :], pin[i % 2][:, :], 1e-36, None, ALU.max).then_inc(s["guarded"], 1)
                pool.wait_ge(s["guarded"], i + 2)
                pool.tensor_tensor(prt[i % 2][:, :], pgd[:, :], half12[:, :], ALU.pow).then_inc(s["roots"], 1)

            def scatter(u):
                pool.wait_ge(s["placed"], u + 1)
                pool.wait_ge(s["x1"], u + 1)
                for k in range(NT):
                    pool.indirect_dma_start(
                        out=rows[:, :], out_offset=bass.IndirectOffsetOnAxis(ap=place[u % 4][:, k:k + 1], axis=0),
                        in_=R[u % 4][:, k, :], in_offset=None).then_inc(scattered[u % 4], 16)

            for i in range(-1, NU + 3):
                if i < NU + 2:
                    roots(i)
                if i >= 3:
                    scatter(i - 3)

            def token(count, k):
                pool.wait_ge(row_loaded[k], count(1) * 16)
                pool.nop().then_inc(seen, 1)
                after(pool, stored[k], count(0) * 16)
                pool.nop().then_inc(seen, 1)
                pool.tensor_copy(tok[k][:, :], XR[k][:, D + 2:D + 3].bitcast(I32)).then_inc(every["token"], 1)

            def store(count, k):
                pool.wait_ge(every["token"], blocks(count(0), k))
                pool.wait_ge(every["out"], blocks(count(0), k))
                pool.nop().then_inc(seen, 1)
                pool.indirect_dma_start(
                    out=out[:, :], out_offset=bass.IndirectOffsetOnAxis(ap=tok[k][:, 0:1], axis=0),
                    in_=OUT[k][:, :], in_offset=None, bounds_check=T - 1, oob_is_err=False).then_inc(stored[k], 16)

            steps(pool, [(-1, store), (3, token)])

        @block.tensor
        def _(pe):
            pe.wait_ge(s["guided"], 1)
            pe.wait_ge(ld["cst"], 16)
            pe.transpose(log_ps[:, 128:128 + G], gdn[:, :], ident[0:G, 0:G]).then_inc(s["guideT_ps"], 1)

            def infl(u):
                pe.wait_ge(s["ET"], u + 1)
                if u >= 1:
                    pe.wait_ge(s["V"], u)
                for k in range(NT):
                    m = pe.matmul(half(infl_ps, k), ET[u % 2][:, k * P:(k + 1) * P], gdz[:, :], start=True, stop=True)
                m.then_inc(s["infl_ps"], 1)

            def xT_(u):
                pe.wait_ge(s["x1"], u + 1)
                if u >= 1:
                    pe.wait_ge(s["xT_sb"], u)
                for k in range(NT):
                    m = pe.transpose(xT_ps[:, k * P:(k + 1) * P], R[u % 4][:, k, 0:D], ident)
                m.then_inc(s["xT_ps"], 1)

            def nT_(u):
                pe.wait_ge(s["n"], u + 1)
                if u >= 1:
                    pe.wait_ge(s["nT_sb"], u)
                for k in range(NT):
                    m = pe.transpose(nT_ps[:, k * P:(k + 1) * P], N[u % 2][:, k, :], ident)
                m.then_inc(s["nT_ps"], 1)

            def traj(u):
                pe.wait_ge(s["V"], u + 1)
                if u >= 1:
                    pe.wait_ge(s["y"], u)
                for k in range(NT):
                    for a in range(2):
                        m = pe.matmul(half(traj_ps, k), band[a][k % 2], V[u % 3][:, 2 * (k // 2) + a, :],
                                      start=a == 0, stop=a == 1)
                m.then_inc(s["traj_ps"], 1)

            def logits(u):
                pe.wait_ge(s["xT_sb"], u + 1)
                if u == 0:
                    pe.wait_ge(s["guideT"], 1)
                    pe.wait_ge(ld["small"], 64)
                if u >= 1:
                    pe.wait_ge(s["placed"], u)
                if u == 3:
                    pe.wait_ge(s["scales_w"], 1)
                for k in range(NT):
                    m = pe.matmul(log_ps[:, k * E:(k + 1) * E], xT[:, k * P:(k + 1) * P], Wr[:, :], start=True, stop=True)
                m.then_inc(s["logits_ps"], 1)

            def sims(u):
                pe.wait_ge(s["nT_sb"], u + 1)
                if u == 0:
                    pe.wait_ge(s["guideT"], 1)
                if u >= 1:
                    pe.wait_ge(s["ET"], u)
                pe.matmul(sims_ps[0:G, :], gdT[:, :], nT[:, :], start=True, stop=True).then_inc(s["sims_ps"], 1)

            def rank(u):
                pe.wait_ge(s["onehot"], u + 1)
                pe.matmul(rank_ps, lt16[:, :], oh16[:, :, :], start=True, stop=False)
                pe.matmul(rank_ps, ones16[:, :], carry16[:, :].unsqueeze(1).to_broadcast([P, NT, E]), start=False, stop=False)
                for k in range(1, NT):
                    m = pe.matmul(rank_ps[:, k * E:], ones16[:, :], oh16[:, 0:NT - k, :], start=False, stop=k == NT - 1)
                m.then_inc(s["rank_ps"], 1)

            for i in range(0, NU + 3):
                if 1 <= i <= NU:
                    infl(i - 1)
                if i >= 3:
                    xT_(i - 3)
                if i < NU:
                    nT_(i)
                if i >= 3:
                    logits(i - 3)
                if i < NU:
                    sims(i)
                if 1 <= i <= NU:
                    traj(i - 1)
                if i >= 3:
                    rank(i - 3)
                if i == 5:
                    pe.wait_ge(s["maxima"], 1)
                    pe.wait_ge(s["placed"], 3)
                    pe.transpose(log_ps[0:4, 128:128 + P], mx[:, 0:4], ident).then_inc(s["maxT_ps"], 1)
                    pe.wait_ge(s["max4"], 1)
                    pe.matmul(log_ps[:, 256:260], ones[0:4, :], mx4[:, 0:4], start=True, stop=True).then_inc(s["maxb_ps"], 1)
            pe.wait_ge(s["counted"], NU)
            pe.matmul(log_ps[:, 300:300 + E], ones16[:, :], carry16[:, :], start=True, stop=True).then_inc(s["tot_ps"], 1)

            pe.wait_ge(s["table"], 1)

            def b_xT(count, k):
                pe.wait_ge(t["xs"][k], count(1))
                pe.transpose(bank[7 * (k % 2)][:, 0:P], xs[k][:, :], ident).then_inc(every["xT_ps"], 1)

            expert = [None] * UN

            def load_expert(count, k):
                return nc.values_load(blk_e[0:1, bass.ds(count(0) * UN + k, 1)], engines=(mybir.EngineType.PE,), min_val=0, max_val=E - 1,
                                      skip_runtime_bounds_check_because="the table is clamped to these bounds")

            def b_h(count, k):
                e = expert[k] = load_expert(count, k)
                sel = sel16[:, bass.ds(count(0) * UN + k, 1)].to_broadcast([96, P])
                pe.wait_ge(t["xl"][k], count(1))
                for c in range(FC):
                    h = bank[1 + k % 4][:, c * P:(c + 1) * P]
                    pe.matmul(h, bias3[:, c * P:(c + 1) * P], sel, start=True, stop=False)
                    wh, wl = W1h[:, bass.ds(e * FF + c * P, P)], W1l[:, bass.ds(e * FF + c * P, P)]
                    pe.matmul(h, wh, xh[k][:, :], start=False, stop=False)
                    pe.matmul(h, wh, xl[k][:, :], start=False, stop=False)
                    m = pe.matmul(h, wl, xh[k][:, :], start=False, stop=True)
                m.then_inc(every["h_ps"], 1)

            def b_y(count, k):
                e = load_expert(count, k) if k == 0 else expert[k]
                y = bank[5 + k % 2]
                pe.wait_ge(t["hl"][k], count(1))
                for c in range(FC):
                    w = W2hl[:, bass.ds(e * FC + c, 1), :]
                    pe.matmul(y[:, 0:2 * D], hh[k][:, c * P:(c + 1) * P], w, start=c == 0, stop=False)
                    if c == 0:
                        pe.matmul(y[:, 0:D], sel16[:, bass.ds(count(0) * UN + k, 1)].to_broadcast([96, P]), bias3[:, FF:FF + D], start=False, stop=False)
                    m = pe.matmul(y[:, 0:D], hl[k][:, c * P:(c + 1) * P], W2hl[:, bass.ds(e * FC + c, 1), 0:D], start=False, stop=c == FC - 1)
                m.then_inc(every["y_ps"], 1)

            steps(pe, [(1, b_h), (3, b_xT), (0, b_y)])

        @block.scalar
        def _(act):
            act.dma_start(gd[:, :], guide).then_inc(ld["guide"], 16)
            act.dma_start(Wr[:, :], wr).then_inc(ld["small"], 16)
            act.dma_start(brb[:, :], br.rearrange("(a e) -> a e", a=1).to_broadcast([P, E])).then_inc(ld["small"], 16)
            act.dma_start(gb[:, 0:1], ln_g.rearrange("(d a) -> d a", a=1)).then_inc(ld["small"], 16)
            act.dma_start(gb[:, 1:2], ln_b.rearrange("(d a) -> d a", a=1)).then_inc(ld["small"], 16)
            act.wait_ge(s["guide_sq"], 1)
            act.activation(gst[:, 1:2], gst[:, 0:1], ACT.Sqrt).then_inc(s["guide_norm"], 1)
            act.wait_ge(s["zeroed"], 1)
            act.activation(warm[:, 0:1], epsc[:, :], ACT.Tanh)

            def sumsq(u):
                act.wait_ge(s["diff"], u + 1)
                for k in range(NT):
                    a = act.activation(sq[:, :], Dd[u % 3][:, k // 2, k % 2, :], ACT.Square, accum_out=pin[(u - 1) % 2][:, k:k + 1])
                    act.drain()
                act.nop().then_inc(s["sumsq"], 1)

            def tanh(u):
                act.wait_ge(s["mags"], u + 1)
                act.activation(st[u % 3][:, MT, :], st[u % 3][:, MAG, :], ACT.Tanh, scale=2.0).then_inc(s["tanh"], 1)

            def np_(u):
                act.wait_ge(s["scales"], u + 1)
                if u >= 3:
                    act.wait_ge(s["traj_ps"], u - 2)
                for k in range(NT):
                    act.activation(V[u % 3][:, k, 0:D], Dd[u % 3][:, k // 2, k % 2, :], ACT.Identity, scale=st[u % 3][:, CN, k:k + 1])
                act.activation(V[u % 3][:, :, D], st[u % 3][:, MT, :], ACT.Identity).then_inc(s["np"], 1)

            def nT_(u):
                act.wait_ge(s["nT_ps"], u + 1)
                if u >= 1:
                    act.wait_ge(s["sims_ps"], u)
                act.activation(nT[:, :], nT_ps[:, :], ACT.Identity).then_inc(s["nT_sb"], 1)

            def et(u):
                act.wait_ge(s["sims_ps"], u + 1)
                if u >= 2:
                    act.wait_ge(s["infl_ps"], u - 1)
                act.activation(ET[u % 2][:, :], sims_ps[0:G, :], ACT.Exp, scale=2.0).then_inc(s["ET"], 1)

            def x1(u):
                act.wait_ge(s["x1c"], u + 1)
                for k in range(NT):
                    a = act.activation(R[u % 4][:, k, 0:D], Y[u % 2][:, k, :], ACT.Identity,
                                       scale=st[u % 3][:, R1, k:k + 1], bias=st[u % 3][:, WR, k:k + 1])
                a.then_inc(s["x1"], 1)

            def xT_(u):
                act.wait_ge(s["xT_ps"], u + 1)
                if u >= 1:
                    act.wait_ge(s["logits_ps"], u)
                act.activation(xT[:, :], xT_ps[:, :], ACT.Identity).then_inc(s["xT_sb"], 1)

            def rexp(u):
                act.wait_ge(s["shifted"], u + 1)
                act.activation(ex[:, :, :], lg[:, :, :], ACT.Exp).then_inc(s["exped"], 1)

            def weights_hi(q):
                act.wait_ge(s["scales_w"], 1)
                e = 2 * q
                act.activation(W1h[:, e * FF:(e + 2) * FF], W1[:, e:e + 2, :], ACT.Identity, scale=scl[:, 1:2])
                act.activation(W2hl[:, e * FC:(e + 2) * FC, 0:D], W2[:, e:e + 2, :, :], ACT.Identity,
                               scale=scl[:, 2:3]).then_inc(s["split_hi"], 1)

            for i in range(-2, NU + 3):
                if i >= 3:
                    xT_(i - 3)
                if 0 <= i < NU:
                    nT_(i)
                    et(i)
                if i + 2 < NU:
                    sumsq(i + 2)
                if i >= 3:
                    rexp(i - 3)
                if 0 <= i + 1 < NU:
                    tanh(i + 1)
                    np_(i + 1)
                if 2 <= i <= NU + 1:
                    x1(i - 2)
                if 6 <= i < 10:
                    weights_hi(i - 6)

            act.wait_ge(s["pad_rows"], 1)
            pads(act, mybir.EngineType.Activation, range(E // 2, E))
            act.activation(warm[:, 1:2], epsc[:, :], ACT.Sqrt)

            def b_xs(count, k):
                act.wait_ge(row_loaded[k], count(1) * 16)
                after(act, every["z0"], blocks(count(-1), k))
                act.activation(cg[k][:, :], XR[k][:, D:D + 1], ACT.Identity, scale=scl[:, 3:4])
                act.activation(xs[k][:, :], XR[k][:, 0:D], ACT.Identity, scale=XR[k][:, D + 1:D + 2]).then_inc(t["xs"][k], 1)

            def b_xt(count, k):
                act.wait_ge(every["xT_ps"], blocks(count(0), k))
                act.activation(xt[k][:, :], bank[7 * (k % 2)][:, 0:P], ACT.Identity, scale=gbs[:, 0:1], bias=gbs[:, 1:2]).then_inc(every["xt"], 1)

            def b_xh(count, k):
                act.wait_ge(every["xt"], blocks(count(0), k))
                act.activation(xh[k][:, :], xt[k][:, :], ACT.Identity).then_inc(t["xh"][k], 1)

            def b_hh(count, k):
                act.wait_ge(every["h_ps"], blocks(count(0), k))
                act.activation(hh[k][:, :], bank[1 + k % 4][:, :], ACT.Relu).then_inc(every["hh"], 1)

            def b_sd(count, k):
                after(act, stored[k], count(0) * 16)
                act.wait_ge(every["mv"], blocks(count(0), k))
                act.activation(sd[k][:, 0:1], mv2[k][:, 1:2], ACT.Sqrt, bias=epsc[:, 0:1]).then_inc(every["sd"], 1)

            steps(act, [(4, b_xs), (1, b_hh), (3, b_xt), (-1, b_sd), (3, b_xh)])

        @block.vector
        def _(dve):
            tt, ts, stt = dve.tensor_tensor, dve.tensor_scalar, dve.scalar_tensor_tensor

            dve.wait_ge(ld["guide"], 16)
            dve.wait_ge(s["zeroed"], 1)
            tt(gdn[:, :], gd[:, :], gd[:, :], ALU.mult)
            ts(gdz[:, 0:D], gd[:, :], GUIDE, None, ALU.mult)
            dve.drain()
            dve.tensor_reduce(gst[:, 0:1], gdn[:, :], AX.X, ALU.add).then_inc(s["guide_sq"], 1)
            dve.wait_ge(s["guide_norm"], 1)
            ts(gst[:, 2:3], gst[:, 1:2], EPS_COS, None, ALU.max)
            dve.drain()
            dve.reciprocal(gst[:, 3:4], gst[:, 2:3])
            dve.drain()
            ts(gdn[:, :], gd[:, :], gst[:, 3:4], None, ALU.mult).then_inc(s["guided"], 1)
            dve.wait_ge(s["guideT_ps"], 1)
            dve.tensor_copy(gdT[:, :], log_ps[:, 128:128 + G]).then_inc(s["guideT"], 1)
            dve.wait_ge(ld["cst"], 16)
            dve.tensor_copy(lt16[:, :], C[:, C_LT:C_LT + P])

            def diff(u):
                g = [0, 1, 1, 2, 2, 3, 3, 3][u]
                dve.wait_ge(ld[f"x{g}"], 32 if g < 3 else 64)
                if u >= 3:
                    dve.wait_ge(s["np"], u - 2)
                b = slice(2 * u, 2 * u + 2)
                tt(Dd[u % 3][:, :, 0, :], X[:, b, 1, :], X[:, b, 0, :], ALU.subtract)
                tt(Dd[u % 3][:, :, 1, :], XN[:, b, :], X[:, b, 1, :], ALU.subtract).then_inc(s["diff"], 1)

            def blend(u):
                q, zi = st[u % 3][:, Q, :], st[u % 3][:, ZI, :]
                dve.wait_ge(s["infl_ps"], u + 1)
                for h in range(2):
                    dve.reciprocal(zi[:, 2 * h:2 * h + 2].unsqueeze(2), pair(infl_ps[h])[:, :, D:D + 1])
                dve.drain()
                tt(q, zi, st[u % 3][:, MT, :], ALU.mult)
                dve.drain()
                dve.wait_ge(s["np"], u + 1)
                for k in range(NT):
                    a = stt(V[u % 3][:, k, 0:D], half(infl_ps, k)[:, 0:D], q[:, k:k + 1], V[u % 3][:, k, 0:D], ALU.mult, ALU.add)
                a.then_inc(s["V"], 1)

            def norm1(u):
                wi = st[u % 3][:, WI, :]
                dve.wait_ge(s["traj_ps"], u + 1)
                for h in range(2):
                    ts(wi[:, 2 * h:2 * h + 2].unsqueeze(2), pair(traj_ps[h])[:, :, D:D + 1], EPS_WSUM, None, ALU.max)
                dve.drain()
                dve.reciprocal(st[u % 3][:, SS, :], wi)
                dve.drain()
                if u >= 2:
                    dve.wait_ge(s["x1"], u - 1)
                for k in range(NT):
                    a = stt(Y[u % 2][:, k, :], half(traj_ps, k)[:, 0:D], st[u % 3][:, SS, k:k + 1], X[:, 2 * u + k // 2, k % 2, :],
                            ALU.mult, ALU.add)
                a.then_inc(s["y"], 1)
                dve.drain()
                for k in range(NT):
                    dve.bn_stats(bn[:, k, :], Y[u % 2][:, k, :])
                dve.drain()
                for k in range(NT):
                    dve.bn_aggr(mv[u % 2][:, k, :], bn[:, k, :])
                dve.drain()
                vp = pin[u % 2]
                ts(vp[:, 4:8], mv[u % 2][:, :, 1], LN_EPS, None, ALU.add)
                dve.drain()
                dve.reciprocal(st[u % 3][:, WI, :], vp[:, 4:8])
                dve.drain()
                tt(st[u % 3][:, VP, :], mv[u % 2][:, :, 1], st[u % 3][:, WI, :], ALU.mult)
                dve.drain()
                ts(vp[:, 8:12], st[u % 3][:, VP, :], LN_EPS, None, ALU.add)

            def moments(i):
                if i + 1 < NU:
                    dve.wait_ge(s["sumsq"], i + 2)
                dve.drain().then_inc(s["moments_in"], 1)

            def router(u):
                dve.wait_ge(s["logits_ps"], u + 1)
                if u == 0:
                    dve.wait_ge(ld["small"], 64)
                tt(lg[:, :, :], log_ps[:, 0:NT * E].rearrange("p (k e) -> p k e", k=NT), brb[:, :].unsqueeze(1).to_broadcast([P, NT, E]), ALU.add)
                dve.drain()
                dve.tensor_reduce(rt[:, 0, :], lg[:, :, :], AX.X, ALU.max)
                dve.drain()
                tt(lg[:, :, :], lg[:, :, :], rt[:, 0, :].unsqueeze(2).to_broadcast([P, NT, E]), ALU.subtract).then_inc(s["shifted"], 1)
                dve.drain()
                stt(oh[:, :, :], lg[:, :, :], 0.0, C[:, C_REV:C_REV + E].unsqueeze(1).to_broadcast([P, NT, E]), ALU.is_ge, ALU.mult)
                dve.drain()
                dve.tensor_reduce(rt[:, 1, :], oh[:, :, :], AX.X, ALU.max)
                dve.drain()
                tt(oh[:, :, :], oh[:, :, :], rt[:, 1, :].unsqueeze(2).to_broadcast([P, NT, E]), ALU.is_equal)
                dve.drain()
                dve.tensor_copy(oh16[:, :, :], oh[:, :, :]).then_inc(s["onehot"], 1)

            def placing(u):
                dve.wait_ge(s["rank_ps"], u + 1)
                if u >= 4:
                    dve.wait_ge(scattered[u % 4], 16 * NT * (u // 4))
                tt(pl[:, :, :], rank_ps.rearrange("p (k e) -> p k e", k=NT), C[:, C_REG:C_REG + E].unsqueeze(1).to_broadcast([P, NT, E]), ALU.add)
                dve.tensor_reduce(cnt[:, :], oh[:, :, :].rearrange("p k e -> p e k"), AX.X, ALU.add)
                dve.wait_ge(s["exped"], u + 1)
                dve.tensor_reduce(rt[:, 2, :], ex[:, :, :], AX.X, ALU.add)
                dve.drain()
                dve.reciprocal(R[u % 4][:, :, D], rt[:, 2, :])
                tt(pl[:, :, :], pl[:, :, :], oh[:, :, :], ALU.mult)
                tt(carry[:, :], carry[:, :], cnt[:, :], ALU.add)
                dve.drain()
                dve.tensor_reduce(rt[:, 3, :], pl[:, :, :], AX.X, ALU.add)
                dve.drain()
                dve.tensor_copy(place[u % 4][:, :], rt[:, 3, :]).then_inc(s["placed"], 1)
                dve.tensor_copy(carry16[:, :], carry[:, :]).then_inc(s["counted"], 1)

            def mags(u):
                m = st[u % 3]
                r = prt[(u - 1) % 2]
                dve.wait_ge(s["roots"], u + 1)
                tt(m[:, MAG, :], pin[(u - 1) % 2][:, 0:NT], r[:, 0:NT], ALU.mult)
                dve.drain()
                stt(m[:, INV, :], m[:, MAG, :], EPS_MAG, r[:, 0:NT], ALU.is_gt, ALU.mult).then_inc(s["mags"], 1)
                dve.drain()
                if u >= 2:
                    dve.wait_ge(s["nT_ps"], u - 1)
                for k in range(NT):
                    a = ts(N[u % 2][:, k, :], Dd[u % 3][:, k // 2, k % 2, :], m[:, INV, k:k + 1], None, ALU.mult)
                a.then_inc(s["n"], 1)
                dve.wait_ge(s["tanh"], u + 1)
                stt(m[:, CN, :], m[:, MT, :], 1.0 - GUIDE, m[:, INV, :], ALU.mult, ALU.mult).then_inc(s["scales"], 1)

            def center(u):
                r = prt[u % 2]
                dve.wait_ge(s["roots"], u + 4)
                if u >= 4:
                    dve.wait_ge(scattered[u % 4], 16 * NT * (u // 4))
                stt(st[u % 3][:, WR, :], mv[u % 2][:, :, 0], -1.0, r[:, 4:8], ALU.mult, ALU.mult)
                dve.tensor_copy(st[u % 3][:, R1, :], r[:, 4:8])
                dve.tensor_copy(R[u % 4][:, :, D + 1], r[:, 8:12])
                dve.tensor_copy(R[u % 4][:, :, D + 2].bitcast(I32), C[:, C_TOK + u * NT:C_TOK + (u + 1) * NT]).then_inc(s["x1c"], 1)

            def maxima(q):
                if q == 0:
                    dve.wait_ge(ld["w1"], 16)
                    dve.wait_ge(ld["w2"], 16)
                dve.tensor_reduce(mx[:, 4 + q:5 + q], W1[:, 2 * q:2 * q + 2, :], AX.XY, ALU.max, apply_absolute_value=True)
                dve.tensor_reduce(mx[:, 8 + q:9 + q], W2[:, 2 * q:2 * q + 2, :, :], AX.XYZ, ALU.max, apply_absolute_value=True)
                if q == 3:
                    dve.wait_ge(ld["bias"], 96)
                    dve.drain()
                    stt(mx[:, 12:14], gb[:, :], -1.0, gb[:, :], ALU.mult, ALU.max)
                    dve.tensor_reduce(mx[:, 1:2], mx[:, 4:8], AX.X, ALU.max)
                    dve.tensor_reduce(mx[:, 2:3], mx[:, 8:12], AX.X, ALU.max)
                    dve.tensor_reduce(mx[0:96, 3:4], bias[:, 0:FF], AX.X, ALU.max, apply_absolute_value=True)
                    dve.drain()
                    stt(mx[:, 0:1], mx[:, 12:13], 11.5, mx[:, 13:14], ALU.mult, ALU.add).then_inc(s["maxima"], 1)

            def scales():
                dve.wait_ge(s["maxT_ps"], 1)
                dve.tensor_reduce(mx4[:, 4:5], log_ps[0:4, 128:128 + P], AX.X, ALU.max)
                dve.drain()
                ts(mx4[:, 0:4], ident[0:4, 0:4], mx4[:, 4:5], None, ALU.mult).then_inc(s["max4"], 1)
                dve.wait_ge(s["maxb_ps"], 1)
                LO = 2.0 ** -40
                v = scl[:, 8:12]
                ts(v, log_ps[:, 256:260], LO, None, ALU.max)
                dve.drain()

                def power(dst, src, k):
                    ts(dst.bitcast(I32), src.bitcast(I32), POW2_MASK, None, ALU.bitwise_and)
                    dve.drain()
                    ts(dst.bitcast(I32), dst.bitcast(I32), -1.0, float((254 + k) << 23), ALU.mult, ALU.add)
                    dve.drain()

                power(scl[:, 0:1], v[:, 0:1], 5)
                power(scl[:, 2:3], v[:, 2:3], 8)
                tt(scl[:, 12:13], v[:, 3:4], scl[:, 0:1], ALU.mult)
                ts(scl[:, 13:14], v[:, 1:2], 0.5, None, ALU.mult)
                dve.drain()
                stt(scl[:, 14:15], scl[:, 12:13], 2.0 ** -13, scl[:, 13:14], ALU.mult, ALU.max)
                dve.drain()
                power(scl[:, 1:2], scl[:, 14:15], 0)
                tt(scl[:, 4:5], scl[:, 0:1], scl[:, 1:2], ALU.mult)
                dve.drain()
                tt(scl[:, 5:6], scl[:, 4:5], scl[:, 2:3], ALU.mult)
                ts(gbs[:, :], gb[:, :], scl[:, 0:1], None, ALU.mult)
                dve.drain()
                power(scl[:, 3:4], scl[:, 5:6], 0)
                ts(bias[:, 0:FF], bias[:, 0:FF], scl[0:96, 4:5], None, ALU.mult)
                ts(bias[:, FF:FF + D], bias[:, FF:FF + D], scl[0:96, 5:6], None, ALU.mult).then_inc(s["scales_w"], 1)

            def split_bias():
                dve.tensor_copy(bias_h[:, :], bias[:, :])
                dve.drain()
                tt(bias_r[:, :], bias[:, :], bias_h[:, :], ALU.subtract)
                dve.drain()
                dve.tensor_copy(bias_m[:, :], bias_r[:, :])
                dve.drain()
                tt(bias_l[:, :], bias_r[:, :], bias_m[:, :], ALU.subtract)
                dve.tensor_copy(bias3[0:32, :], bias_h[0:32, :])
                dve.tensor_copy(bias3[32:64, :], bias_m[32:64, :])
                dve.drain()
                dve.tensor_copy(bias3[64:96, :], bias_l[64:96, :])

            def split_lo(q):
                dve.wait_ge(s["split_hi"], q + 1)
                e2 = slice(2 * q * FF, (2 * q + 2) * FF)
                stt(W1l[:, e2].rearrange("p (e f) -> p e f", e=2), W1[:, 2 * q:2 * q + 2, :], scl[:, 1:2],
                    W1h[:, e2].rearrange("p (e f) -> p e f", e=2), ALU.mult, ALU.subtract)
                w = W2hl[:, 2 * q * FC:(2 * q + 2) * FC, :]
                stt(w[:, :, D:2 * D], W2[:, 2 * q:2 * q + 2, :, :].rearrange("p e c d -> p (e c) d"), scl[:, 2:3], w[:, :, 0:D], ALU.mult, ALU.subtract)

            for i in range(-2, NU + 3):
                if 2 <= i <= NU + 1:
                    norm1(i - 2)
                if -1 <= i <= NU + 1:
                    moments(i)
                if 1 <= i <= NU:
                    blend(i - 1)
                if i + 2 < NU:
                    diff(i + 2)
                if i >= 3:
                    router(i - 3)
                if 1 <= i < 5:
                    maxima(i - 1)
                if i == 6:
                    split_bias()
                if 7 <= i < 11:
                    split_lo(i - 7)
                if i >= 3:
                    placing(i - 3)
                if 0 <= i + 1 < NU:
                    mags(i + 1)
                if 2 <= i <= NU + 1:
                    center(i - 2)
                if i == 5:
                    scales()

            dve.wait_ge(s["tot_ps"], 1)
            dve.tensor_copy(tot[:, :], log_ps[:, 300:300 + E])
            dve.drain()
            ts(nblk_i[:, :], tot[:, :], float(P - 1), None, ALU.add)
            tt(pad_row[:, :], tot[:, :], C[:, C_REG:C_REG + E], ALU.add)
            dve.drain()
            ts(nblk_i[:, :], nblk_i[:, :], 7, None, ALU.arith_shift_right)
            dve.drain().then_inc(s["pad_rows"], 1)
            dve.tensor_copy(nblk[:, :], nblk_i[:, :])
            dve.drain()
            dve.tensor_tensor_scan(cend[:, :], ones[:, 0:E], nblk[:, :], 0.0, ALU.mult, ALU.add)
            ts(jump[:, :], nblk[:, :], -float(P), float(REG), ALU.mult, ALU.add)
            dve.drain()
            tt(past[:, :, :], cend[:, :].unsqueeze(1).to_broadcast([P, NB, E]),
               C[:, C_BLK:C_BLK + NB].unsqueeze(2).to_broadcast([P, NB, E]), ALU.is_le)
            dve.drain()
            dve.tensor_reduce(blk[:, 0, :], past[:, :, :], AX.X, ALU.add)
            tt(past2[:, :, :], past[:, :, :], jump[:, :].unsqueeze(1).to_broadcast([P, NB, E]), ALU.mult)
            dve.drain()
            dve.tensor_reduce(blk[:, 1, :], past2[:, :, :], AX.X, ALU.add)
            ts(blk[:, 0, :], blk[:, 0, :], float(E - 1), None, ALU.min)
            dve.drain()
            stt(blk[:, 2, :], C[:, C_BLK:C_BLK + NB], float(P), blk[:, 1, :], ALU.mult, ALU.add)
            dve.tensor_copy(blk_e[:, :], blk[:, 0, :])
            ts(sel16[:, :], blk[0:96, 0, :], C[0:96, C_EID:C_EID + 1], None, ALU.is_equal)
            dve.drain()
            ts(blk_row[:, :], blk[:, 2, :], float(PADROW), None, ALU.min)
            dve.drain().then_inc(s["table"], 1)

            def b_xl(count, k):
                dve.wait_ge(t["xh"][k], count(1))
                tt(xl[k][:, :], xt[k][:, :], xh[k][:, :], ALU.subtract).then_inc(t["xl"][k], 1)

            def b_hl(count, k):
                dve.wait_ge(every["hh"], blocks(count(0), k))
                stt(hl[k][:, :], bank[1 + k % 4][:, :], 0.0, hh[k][:, :], ALU.max, ALU.subtract).then_inc(t["hl"][k], 1)

            def b_z0(count, k):
                dve.wait_ge(every["y_ps"], blocks(count(0), k))
                stt(z0[k][:, :], bank[5 + k % 2][:, 0:D], cg[k][:, :], XR[k][:, 0:D], ALU.mult, ALU.add).then_inc(every["z0"], 1)

            def b_z(count, k):
                dve.wait_ge(every["z0"], blocks(count(0), k))
                stt(z[k][:, :], bank[5 + k % 2][:, D:2 * D], cg[k][:, :], z0[k][:, :], ALU.mult, ALU.add).then_inc(t["z"][k], 1)

            def b_bn(count, k):
                dve.wait_ge(t["z"][k], count(1))
                dve.bn_stats(bn2[k][:, :], z[k][:, :])

            def b_mv(count, k):
                dve.drain()
                dve.bn_aggr(mv2[k][:, :], bn2[k][:, :]).then_inc(every["mv"], 1)

            def b_rec(count, k):
                dve.wait_ge(every["sd"], blocks(count(0), k))
                dve.reciprocal(sd[k][:, 1:2], sd[k][:, 0:1]).then_inc(every["rec"], 1)

            def b_fin(count, k):
                dve.wait_ge(every["rec"], blocks(count(0), k))
                ts(OUT[k][:, :], z[k][:, :], mv2[k][:, 0:1], sd[k][:, 1:2], ALU.subtract, ALU.mult).then_inc(every["out"], 1)

            steps(dve, [(1, b_hl), (0, b_z0), (-1, b_rec), (0, b_z), (-1, b_fin), (0, b_bn), (3, b_xl), (0, b_mv)])


def kernel(**inputs):
    import concourse.bacc as bacc
    from concourse.bass_utils import run_bass_kernel_spmd

    nc = bacc.Bacc("TRN2", target_bir_lowering=False, num_devices=1)
    arrays, aps = {}, []
    names = ("attn_embeddings", "attn_guidance_trajectories", "ffn_Wr", "ffn_br", "ffn_ln_g", "ffn_ln_b",
             "ffn_W1", "ffn_b1", "ffn_W2", "ffn_b2")
    for name in names:
        a = np.ascontiguousarray(inputs["L0_" + name])
        arrays["in_" + name] = a
        aps.append(nc.dram_tensor("in_" + name, a.shape, mybir.dt.from_np(a.dtype), kind="ExternalInput").ap())
    arrays["in_constants"] = constants()
    aps.append(nc.dram_tensor("in_constants", (P, C_N), F32, kind="ExternalInput").ap())
    rows = nc.dram_tensor("rows", (PADROW + P, ROW), F32, kind="Internal").ap()
    out = nc.dram_tensor("out", (T, D), F32, kind="ExternalOutput").ap()
    build(nc, *aps, rows, out)
    r = run_bass_kernel_spmd(nc, [arrays], core_ids=[0])
    return r.results[0]["out"].reshape(B, S, D)
```

```python
from contextlib import ExitStack

import numpy as np

import concourse.bass as bass
from concourse import mybir

F32 = mybir.dt.float32
F16 = mybir.dt.float16
BF16 = mybir.dt.bfloat16
I32 = mybir.dt.int32
ALU = mybir.AluOpType
ACT = mybir.ActivationFunctionType
AX = mybir.AxisListType

P = 128
B, S, D = 16, 256, 128
T = B * S
E, FF = 8, 512
FC = FF // P
G = 64
W = 8
NT = 4
NU = T // (NT * P)
REG = T + P
PADROW = E * REG
NB = (T + E * (P - 1)) // P
ROW = D + 4
UN = 8
LN_EPS = 1e-5
EPS_MAG, EPS_COS, EPS_WSUM, GUIDE = 1e-6, 1e-8, 1e-8, 0.4
POW2_MASK = 0x7F800000

C_BAND = 0
C_ID = C_BAND + 4 * P
C_LT = C_ID + P
C_REG = C_LT + P
C_REV = C_REG + E
C_BLK = C_REV + E
C_TOK = C_BLK + NB
C_EID = C_TOK + NU * NT
C_N = C_EID + 1


def constants():
    c = np.zeros((P, C_N), np.float32)
    for s in range(1, S):
        w = min(s, W)
        for j in range(w):
            i = s - w + j
            v = np.float32(0.1) + np.float32(0.9) * np.float32(j) / np.float32(max(w - 1, 1)) if w > 1 else 0.1
            c[i // 2, C_BAND + (2 * (i % 2) + s % 2) * P + s // 2] = v
    c[:, C_ID:C_ID + P] = np.eye(P)
    c[:, C_LT:C_LT + P] = np.triu(np.ones((P, P)), 1)
    c[:, C_REG:C_REG + E] = np.arange(E) * REG
    c[:, C_REV:C_REV + E] = E - np.arange(E)
    c[:, C_BLK:C_BLK + NB] = np.arange(NB)
    p = np.arange(P)
    for u in range(NU):
        for k in range(NT):
            c[:, C_TOK + u * NT + k] = (2 * u + k // 2) * S + 2 * p + k % 2
    c[:, C_EID] = np.where((p % 32 < E) & (p < 96), p % 32, -1)
    return c


def build(nc, x, guide, wr, br, ln_g, ln_b, w1, b1, w2, b2, cst, rows, out):
    with ExitStack() as ctx:
        def sb(name, shape, dt=F32):
            return ctx.enter_context(nc.sbuf_tensor(name, shape, dt))

        def sem(name):
            return ctx.enter_context(nc.semaphore(name))

        bank = [ctx.enter_context(nc.psum_tensor(f"bank{i}", [P, 512], F32)) for i in range(8)]

        C = sb("C", [P, C_N])
        lt16 = sb("lt16", [P, P], BF16)
        ones16 = sb("ones16", [P, P], BF16)
        ones = sb("ones", [P, P])
        gd = sb("gd", [G, D])
        gdn = sb("gdn", [G, D])
        gdT = sb("gdT", [P, G])
        gdz = sb("gdz", [G, D + 1])
        gst = sb("gst", [G, 4])
        epsc = sb("epsc", [P, 1])
        warm = sb("warm", [P, 2])
        Wr = sb("Wr", [P, E])
        brb = sb("brb", [P, E])
        gb = sb("gb", [P, 2])
        gbs = sb("gbs", [P, 2])
        W1 = sb("W1", [P, E, FF])
        W2 = sb("W2", [P, E, FC, D])
        W1h = sb("W1h", [P, E * FF], F16)
        W1l = sb("W1l", [P, E * FF], F16)
        W2hl = sb("W2hl", [P, E * FC, 2 * D], F16)
        bias = sb("bias", [96, FF + D])
        bias_r = sb("bias_r", [96, FF + D])
        bias_m = sb("bias_m", [96, FF + D], BF16)
        bias3 = sb("bias3", [96, FF + D], BF16)
        mx = sb("mx", [P, 16])
        mx4 = sb("mx4", [4, 8])
        scl = sb("scl", [P, 16])

        X = sb("X", [P, B, 2, D])
        XN = sb("XN", [P, B, D])
        Dd = [sb(f"Dd{i}", [P, 2, 2, D]) for i in range(3)]
        sq = sb("sq", [P, D])
        N = [sb(f"N{i}", [P, NT, D]) for i in range(2)]
        V = [sb(f"V{i}", [P, NT, D + 1]) for i in range(3)]
        nT = sb("nT", [P, NT * P])
        ET = [sb(f"ET{i}", [G, NT * P]) for i in range(2)]
        sumsq_in = [sb(f"sumsq_in{i}", [P, NT]) for i in range(2)]
        guarded = sb("guarded", [P, NT])
        rmag = [sb(f"rmag{i}", [P, NT]) for i in range(2)]
        var_in = [sb(f"var_in{i}", [P, 2, NT]) for i in range(2)]
        rstd = [sb(f"rstd{i}", [P, NT]) for i in range(2)]
        minus_half = sb("minus_half", [P, NT])
        st = [sb(f"st{i}", [P, 12, NT]) for i in range(3)]
        Y = [sb(f"Y{i}", [P, NT, D]) for i in range(2)]
        bn = sb("bn", [P, NT, 6])
        mv = [sb(f"mv{i}", [P, NT, 2]) for i in range(2)]
        R = [sb(f"R{i}", [P, NT, ROW]) for i in range(4)]
        xT = sb("xT", [P, NT * P])
        lg = sb("lg", [P, NT, E])
        ex = sb("ex", [P, NT, E])
        oh = sb("oh", [P, NT, E])
        oh16 = sb("oh16", [P, NT, E], BF16)
        carry = sb("carry", [P, E])
        carry16 = sb("carry16", [P, E], BF16)
        rt = sb("rt", [P, 4, NT])
        place = [sb(f"place{i}", [P, NT], I32) for i in range(4)]

        tot = sb("tot", [P, E])
        nblk = sb("nblk", [P, E])
        nblk_i = sb("nblk_i", [P, E], I32)
        pl = sb("pl", [P, NT, E])
        cnt = sb("cnt", [P, E])
        cend = sb("cend", [P, E])
        jump = sb("jump", [P, E])
        past = sb("past", [P, NB, E])
        past2 = sb("past2", [P, NB, E])
        blk = sb("blk", [P, 3, NB])
        blk_e = sb("blk_e", [P, 4 * (-(-NB // 4))], I32)
        blk_row = sb("blk_row", [P, 4 * (-(-NB // 4))], I32)
        pad_row = sb("pad_row", [P, E], I32)
        sel16 = sb("sel16", [96, NB], BF16)
        padt = sb("padt", [P, ROW])

        XR = [sb(f"XR{i}", [P, ROW]) for i in range(UN)]
        tok = [sb(f"tok{i}", [P, 1], I32) for i in range(UN)]
        xs = [sb(f"xs{i}", [P, D]) for i in range(UN)]
        cg = [sb(f"cg{i}", [P, 1]) for i in range(UN)]
        xt = [sb(f"xt{i}", [P, P]) for i in range(UN)]
        xh = [sb(f"xh{i}", [P, P], F16) for i in range(UN)]
        xl = [sb(f"xl{i}", [P, P], F16) for i in range(UN)]
        hh = [sb(f"hh{i}", [P, FF], F16) for i in range(UN)]
        hl = [sb(f"hl{i}", [P, FF], F16) for i in range(UN)]
        z0 = [sb(f"zpart{i}", [P, D]) for i in range(UN)]
        z = [sb(f"z{i}", [P, D]) for i in range(UN)]
        bn2 = [sb(f"bn2{i}", [P, 6]) for i in range(UN)]
        mv2 = [sb(f"mv2{i}", [P, 2]) for i in range(UN)]
        sd = [sb(f"sd{i}", [P, 3]) for i in range(UN)]
        OUT = [sb(f"OUT{i}", [P, D]) for i in range(UN)]

        ld = {n: sem("ld_" + n) for n in ("cst", "guide", "small", "x0", "x1", "x2", "x3", "w1", "w2", "bias")}
        names = ("zeroed diff sumsq guarded rmag var_in rstd var2_in r2 mags tanh scales n np nT_ps nT_sb sims_ps ET "
                 "infl_ps V traj_ps y x1c x1 xT_ps xT_sb logits_ps shifted exped onehot rank_ps placed "
                 "counted guide_sq guide_norm guided guideT_ps guideT split_hi split_lo maxima maxT_ps max4 maxb_ps max_read scales_w "
                 "bias_hi bias_rest tot_ps pad_rows table pads_ready").split()
        s = {n: sem(n) for n in names}
        scattered = [sem(f"scattered{i}") for i in range(4)]
        padded = sem("padded")
        names2 = "xs xh xl hl z".split()
        t = {n: [sem(f"b_{n}{i}") for i in range(UN)] for n in names2}
        every = {n: sem("every_" + n) for n in "token xT_ps xt h_ps hh y_ps z0 bn mv sd rec shift out".split()}
        seen = sem("seen")
        row_loaded = [sem(f"row_loaded{i}") for i in range(UN)]
        stored = [sem(f"stored{i}") for i in range(UN)]

        band = [[C[:, C_BAND + (2 * a + b) * P:C_BAND + (2 * a + b + 1) * P] for b in range(2)] for a in range(2)]
        ident = C[:, C_ID:C_ID + P]
        nT_ps, sims_ps = bank[0], bank[1]
        infl_ps, traj_ps, xT_ps, log_ps = [bank[2], bank[3]], [bank[4], bank[5]], bank[6], bank[7]
        rank_ps = bank[5][:, 300:300 + NT * E]

        def tile_of(banks, k):
            return banks[k // 2][:, (k % 2) * (D + 1):(k % 2 + 1) * (D + 1)]

        def pair(b):
            return b[:, 0:2 * (D + 1)].rearrange("p (k d) -> p k d", k=2)

        block = ctx.enter_context(nc.Block())

        MAG, INV, CN, MT, Q, ZI, WI, SS, RV, VP, WR = range(11)

        LO_AT = (7, 9)
        AHEAD = 1

        def after(eng, signal, count):
            if not isinstance(count, int) or count > 0:
                eng.wait_ge(signal, count)

        def steps(eng, stages, turn_starts=None):
            hi = max(lead for lead, _ in stages)
            lo = min(lead for lead, _ in stages)
            def straight(b0, b1):
                for b in range(b0, b1):
                    for lead, f in stages:
                        if 0 <= b + lead < NB:
                            f(lambda d, turn=(b + lead) // UN: turn + d, (b + lead) % UN)
            turns = (NB - hi) // UN
            if turn_starts:
                turn_starts(0)
            straight(-hi, UN)
            with eng.Fori(1, turns) as turn:
                held = {}
                if turn_starts:
                    turn_starts(turn * UN)
                def count(d):
                    if d not in held:
                        held[d] = eng.snap(turn + d) if d else turn
                    return held[d]
                for k in range(UN):
                    for lead, f in stages:
                        f(lambda d, more=(k + lead) // UN: count(d + more), (k + lead) % UN)
            if turn_starts:
                turn_starts(turns * UN)
            straight(turns * UN, NB - lo)

        def blocks(turn, k):
            return turn * UN + k + 1

        def pads(eng, first, n):
            at = [eng.alloc_register(f"pad_row{e}") for e in range(n)]
            eng.load(at, pad_row[0:1, first:first + n])
            for e in range(n):
                r = eng.snap(at[e], min_val=0, max_val=PADROW - P)
                eng.dma_start(rows[bass.ds(r, P), :], padt[:, :]).then_inc(padded, 16)

        @block.sync
        def _(sp):
            sp.dma_start(X[:, 0:2, :, :], x[0:2].rearrange("b (p c) d -> p b (c d)", c=2).rearrange(
                "p b (c d) -> p b c d", c=2)).then_inc(ld["x0"], 16)
            nxt = x.rearrange("b s d -> (b s) d")
            nv = nxt[2:T, :].rearrange("(n c) d -> n c d", c=2)[:, 0, :]
            def next_rows(b0, b1, which):
                if b1 < B:
                    sp.dma_start(XN[:, b0:b1, :], nv[b0 * P:b1 * P, :].rearrange("(b p) d -> p b d", p=P)).then_inc(ld[which], 16)
                else:
                    sp.dma_start(XN[:, b0:B - 1, :], nv[b0 * P:(B - 1) * P, :].rearrange("(b p) d -> p b d", p=P)).then_inc(ld[which], 16)
                    sp.dma_start(XN[0:P - 1, B - 1, :], nv[(B - 1) * P:B * P - 1, :]).then_inc(ld[which], 16)
                    sp.dma_start(XN[P - 1:P, B - 1, :], nxt[T - 1:T, :]).then_inc(ld[which], 16)
            next_rows(0, 2, "x0")
            sp.dma_start(C[:, :], cst).then_inc(ld["cst"], 16)
            for n, (a, b) in enumerate(((2, 6), (6, 10), (10, 16)), 1):
                sp.dma_start(X[:, a:b, :, :], x[a:b].rearrange("b (p c) d -> p b c d", c=2)).then_inc(ld[f"x{n}"], 16)
                next_rows(a, b, f"x{n}")
                if n == 1:
                    sp.dma_start(W1[:, :, :], w1.rearrange("e d f -> d e f")).then_inc(ld["w1"], 16)
            sp.dma_start(Wr[:, :], wr).then_inc(ld["small"], 16)
            sp.dma_start(brb[:, :], br.rearrange("(a e) -> a e", a=1).to_broadcast([P, E])).then_inc(ld["small"], 16)
            sp.dma_start(gb[:, 0:1], ln_g.rearrange("(d a) -> d a", a=1)).then_inc(ld["small"], 16)
            sp.dma_start(gb[:, 1:2], ln_b.rearrange("(d a) -> d a", a=1)).then_inc(ld["small"], 16)
            sp.dma_start(W2[:, :, :, :], w2.rearrange("e (c p) d -> p e c d", p=P)).then_inc(ld["w2"], 16)
            sp.wait_ge(s["zeroed"], 1)
            for j in range(3):
                sp.dma_start(bias[32 * j:32 * j + E, 0:FF], b1).then_inc(ld["bias"], 16)
                sp.dma_start(bias[32 * j:32 * j + E, FF:FF + D], b2).then_inc(ld["bias"], 16)
            sp.wait_ge(s["pads_ready"], 1)
            sp.dma_start(rows[PADROW:PADROW + P, :], padt[:, :]).then_inc(padded, 16)
            sp.wait_ge(s["pad_rows"], 1)
            pads(sp, 0, E // 2)
            sp.wait_ge(s["table"], 1)
            sp.wait_ge(padded, 16 * (E + 1))
            for i in range(4):
                sp.wait_ge(scattered[i], 16 * NT * (NU // 4))

            held_row = [sp.alloc_register(f"row{i}") for i in range(UN)]
            row = {}

            def load_rows(first):
                n = min(UN, NB - first) if isinstance(first, int) else UN
                sp.load(held_row[0:n], blk_row[0:1, bass.ds(first, n)])
                for j in range(n):
                    row[j] = sp.snap(held_row[j], min_val=0, max_val=PADROW)

            def load(count, k):
                after(sp, every["z0"], blocks(count(-1), k))
                after(sp, every["token"], blocks(count(-1), k))
                sp.dma_start(XR[k][:, :], rows[bass.ds(row[k], P), :]).then_inc(row_loaded[k], 16)

            steps(sp, [(0, load)], load_rows)
            for k in range(UN):
                sp.wait_ge(stored[k], 16 * (NB // UN + (k < NB % UN)))

        @block.gpsimd
        def _(pool):
            pool.memset(bias[:, :], 0.0)
            pool.memset(carry[:, :], 0.0)
            pool.memset(carry16[:, :], 0.0)
            pool.memset(padt[:, :], 0.0)
            pool.memset(mx[:, :], 0.0)
            pool.memset(epsc[:, :], LN_EPS)
            pool.memset(minus_half[:, :], -0.5)
            for i in range(4):
                pool.memset(R[i][:, :, D + 3:D + 4], 0.0)
            pool.memset(ones[:, :], 1.0)
            pool.memset(ones16[:, :], 1.0)
            pool.memset(gdz[:, D:D + 1], 1.0).then_inc(s["zeroed"], 1)
            pool.wait_ge(s["zeroed"], 1)
            pool.memset(padt[:, D + 2:D + 3].bitcast(I32), T).then_inc(s["pads_ready"], 1)

            def mag_roots(u):
                pool.wait_ge(s["sumsq"], u + 1)
                if u >= 1:
                    pool.wait_ge(s["rmag"], u)
                pool.tensor_scalar(guarded[:, :], sumsq_in[u % 2][:, :], 1e-36, None, ALU.max).then_inc(s["guarded"], 1)
                pool.wait_ge(s["guarded"], u + 1)
                if u >= 2:
                    pool.wait_ge(s["mags"], u - 1)
                pool.tensor_tensor(rmag[u % 2][:, :], guarded[:, :], minus_half[:, :], ALU.pow).then_inc(s["rmag"], 1)

            def std_roots(u):
                pool.wait_ge(s["var_in"], u + 1)
                pool.tensor_tensor(rstd[u % 2][:, :], var_in[u % 2][:, 0, :], minus_half[:, :], ALU.pow).then_inc(s["rstd"], 1)
                pool.wait_ge(s["var2_in"], u + 1)
                if u >= 4:
                    pool.wait_ge(scattered[u % 4], 16 * NT * (u // 4))
                pool.tensor_tensor(R[u % 4][:, :, D + 1], var_in[u % 2][:, 1, :], minus_half[:, :], ALU.pow)
                pool.tensor_copy(R[u % 4][:, :, D + 2].bitcast(I32), C[:, C_TOK + u * NT:C_TOK + (u + 1) * NT]).then_inc(s["r2"], 1)

            def scatter(u):
                pool.wait_ge(s["placed"], u + 1)
                pool.wait_ge(s["x1"], u + 1)
                pool.wait_ge(s["r2"], u + 1)
                for k in range(NT):
                    pool.indirect_dma_start(
                        out=rows[:, :], out_offset=bass.IndirectOffsetOnAxis(ap=place[u % 4][:, k:k + 1], axis=0),
                        in_=R[u % 4][:, k, :], in_offset=None).then_inc(scattered[u % 4], 16)

            pool.wait_ge(s["guide_sq"], 1)
            pool.tensor_scalar(gst[:, 1:2], gst[:, 0:1], EPS_COS ** 2, None, ALU.max).then_inc(s["guide_sq"], 1)
            pool.wait_ge(s["guide_sq"], 2)
            pool.tensor_tensor(gst[:, 2:3], gst[:, 1:2], minus_half[0:G, 0:1], ALU.pow).then_inc(s["guide_norm"], 1)
            pool.wait_ge(ld["cst"], 16)
            for i in range(-1, NU + 4):
                if i + 1 < NU:
                    mag_roots(i + 1)
                if 2 <= i <= NU + 1:
                    std_roots(i - 2)
                if i >= 4:
                    scatter(i - 4)

            def token(count, k):
                pool.wait_ge(row_loaded[k], count(1) * 16)
                pool.nop().then_inc(seen, 1)
                after(pool, stored[k], count(0) * 16)
                pool.nop().then_inc(seen, 1)
                pool.tensor_scalar(cg[k][:, :], XR[k][:, D:D + 1], scl[:, 3:4], None, ALU.mult)
                pool.tensor_copy(tok[k][:, :], XR[k][:, D + 2:D + 3].bitcast(I32)).then_inc(every["token"], 1)

            def store(count, k):
                pool.wait_ge(every["token"], blocks(count(0), k))
                pool.wait_ge(every["out"], blocks(count(0), k))
                pool.nop().then_inc(seen, 1)
                pool.indirect_dma_start(
                    out=out[:, :], out_offset=bass.IndirectOffsetOnAxis(ap=tok[k][:, 0:1], axis=0),
                    in_=OUT[k][:, :], in_offset=None, bounds_check=T - 1, oob_is_err=False).then_inc(stored[k], 16)

            steps(pool, [(-3, store), (3, token)])

        @block.tensor
        def _(pe):
            pe.wait_ge(s["guided"], 1)
            pe.wait_ge(ld["cst"], 16)
            pe.transpose(log_ps[:, 128:128 + G], gdn[:, :], ident[0:G, 0:G]).then_inc(s["guideT_ps"], 1)

            def infl(u):
                pe.wait_ge(s["ET"], u + 1)
                if u >= 1:
                    pe.wait_ge(s["V"], u)
                for k in range(NT):
                    m = pe.matmul(tile_of(infl_ps, k), ET[u % 2][:, k * P:(k + 1) * P], gdz[:, :], start=True, stop=True)
                m.then_inc(s["infl_ps"], 1)

            def xT_(u):
                pe.wait_ge(s["x1"], u + 1)
                if u >= 1:
                    pe.wait_ge(s["xT_sb"], u)
                if u == 3:
                    pe.wait_ge(s["max_read"], 1)
                for k in range(NT):
                    m = pe.transpose(xT_ps[:, k * P:(k + 1) * P], R[u % 4][:, k, 0:D], ident)
                m.then_inc(s["xT_ps"], 1)

            def nT_(u):
                pe.wait_ge(s["n"], u + 1)
                if u >= 1:
                    pe.wait_ge(s["nT_sb"], u)
                for k in range(NT):
                    m = pe.transpose(nT_ps[:, k * P:(k + 1) * P], N[u % 2][:, k, :], ident)
                m.then_inc(s["nT_ps"], 1)

            def traj(u):
                pe.wait_ge(s["V"], u + 1)
                if u >= 1:
                    pe.wait_ge(s["y"], u)
                for k in range(NT):
                    for a in range(2):
                        m = pe.matmul(tile_of(traj_ps, k), band[a][k % 2], V[u % 3][:, 2 * (k // 2) + a, :],
                                      start=a == 0, stop=a == 1)
                m.then_inc(s["traj_ps"], 1)

            def logits(u):
                pe.wait_ge(s["xT_sb"], u + 1)
                if u == 0:
                    pe.wait_ge(s["guideT"], 1)
                    pe.wait_ge(ld["small"], 64)
                if u >= 1:
                    pe.wait_ge(s["shifted"], u)
                for k in range(NT):
                    m = pe.matmul(log_ps[:, k * E:(k + 1) * E], xT[:, k * P:(k + 1) * P], Wr[:, :], start=True, stop=True)
                m.then_inc(s["logits_ps"], 1)

            def sims(u):
                pe.wait_ge(s["nT_sb"], u + 1)
                if u == 0:
                    pe.wait_ge(s["guideT"], 1)
                if u >= 1:
                    pe.wait_ge(s["ET"], u)
                pe.matmul(sims_ps[0:G, :], gdT[:, :], nT[:, :], start=True, stop=True).then_inc(s["sims_ps"], 1)

            def rank(u):
                pe.wait_ge(s["onehot"], u + 1)
                if u >= 1:
                    pe.wait_ge(s["counted"], u)
                pe.matmul(rank_ps, lt16[:, :], oh16[:, :, :], start=True, stop=False)
                pe.matmul(rank_ps, ones16[:, :], carry16[:, :].unsqueeze(1).to_broadcast([P, NT, E]), start=False, stop=False)
                for k in range(1, NT):
                    m = pe.matmul(rank_ps[:, k * E:], ones16[:, :], oh16[:, 0:NT - k, :], start=False, stop=k == NT - 1)
                m.then_inc(s["rank_ps"], 1)

            for i in range(0, NU + 3):
                if i == 5:
                    pe.wait_ge(s["maxima"], 1)
                    pe.wait_ge(s["xT_sb"], 3)
                    pe.transpose(xT_ps[0:4, 0:P], mx[:, 0:4], ident).then_inc(s["maxT_ps"], 1)
                if i < NU:
                    nT_(i)
                if i >= 3:
                    logits(i - 3)
                if i < NU:
                    sims(i)
                if i == 5:
                    pe.wait_ge(s["max4"], 1)
                    pe.matmul(xT_ps[:, P:P + 4], ones[0:4, :], mx4[:, 0:4], start=True, stop=True).then_inc(s["maxb_ps"], 1)
                if 1 <= i <= NU:
                    traj(i - 1)
                if i >= 3:
                    rank(i - 3)
                if i < NU:
                    infl(i)
                if 2 <= i <= NU + 1:
                    xT_(i - 2)
            pe.wait_ge(s["counted"], NU)
            pe.matmul(log_ps[:, 300:300 + E], ones16[:, :], carry16[:, :], start=True, stop=True).then_inc(s["tot_ps"], 1)

            pe.wait_ge(s["table"], 1)
            pe.wait_ge(s["split_lo"], 1)

            def b_xT(count, k):
                pe.wait_ge(t["xs"][k], count(1))
                pe.transpose(bank[7 * (k % 2)][:, 0:P], xs[k][:, :], ident).then_inc(every["xT_ps"], 1)

            held_expert = [pe.alloc_register(f"expert{i}") for i in range(UN + AHEAD)]
            expert = {}

            def load_experts(first):
                n = min(UN + AHEAD, NB - first) if isinstance(first, int) else UN + AHEAD
                pe.load(held_expert[0:n], blk_e[0:1, bass.ds(first, n)])
                expert.clear()
                expert["first"] = first
                for j in range(n):
                    expert[j] = pe.snap(held_expert[j], min_val=0, max_val=E - 1)

            def expert_of(count, k, lead):
                if isinstance(count(0), int):
                    return expert[count(0) * UN + k - expert["first"]]
                return expert[k if k >= lead else UN + k]

            def b_h(count, k):
                e = expert_of(count, k, AHEAD)
                sel = sel16[:, bass.ds(count(0) * UN + k, 1)].to_broadcast([96, P])
                pe.wait_ge(t["xl"][k], count(1))
                for c in range(FC):
                    h = bank[1 + k % 4][:, c * P:(c + 1) * P]
                    pe.matmul(h, bias3[:, c * P:(c + 1) * P], sel, start=True, stop=False)
                    wh, wl = W1h[:, bass.ds(e * FF + c * P, P)], W1l[:, bass.ds(e * FF + c * P, P)]
                    pe.matmul(h, wh, xh[k][:, :], start=False, stop=False)
                    pe.matmul(h, wh, xl[k][:, :], start=False, stop=False)
                    m = pe.matmul(h, wl, xh[k][:, :], start=False, stop=True)
                m.then_inc(every["h_ps"], 1)

            def b_y(count, k):
                e = expert_of(count, k, 0)
                y = bank[5 + k % 2]
                pe.wait_ge(t["hl"][k], count(1))
                for c in range(FC):
                    w = W2hl[:, bass.ds(e * FC + c, 1), :]
                    pe.matmul(y[:, 0:2 * D], hh[k][:, c * P:(c + 1) * P], w, start=c == 0, stop=False)
                    if c == 0:
                        pe.matmul(y[:, 0:D], sel16[:, bass.ds(count(0) * UN + k, 1)].to_broadcast([96, P]), bias3[:, FF:FF + D], start=False, stop=False)
                    m = pe.matmul(y[:, 0:D], hl[k][:, c * P:(c + 1) * P], W2hl[:, bass.ds(e * FC + c, 1), 0:D], start=False, stop=c == FC - 1)
                m.then_inc(every["y_ps"], 1)

            steps(pe, [(1, b_h), (4, b_xT), (0, b_y)], load_experts)

        @block.scalar
        def _(act):
            act.dma_start(gd[:, :], guide).then_inc(ld["guide"], 16)
            act.wait_ge(s["zeroed"], 1)
            act.activation(warm[:, 0:1], epsc[:, :], ACT.Tanh)

            def sumsq(u):
                act.wait_ge(s["diff"], u + 1)
                for k in range(NT):
                    a = act.activation(sq[:, :], Dd[u % 3][:, k // 2, k % 2, :], ACT.Square, accum_out=sumsq_in[u % 2][:, k:k + 1])
                    act.drain()
                act.nop().then_inc(s["sumsq"], 1)

            def tanh(u):
                act.wait_ge(s["mags"], u + 1)
                act.activation(st[u % 3][:, MT, :], st[u % 3][:, MAG, :], ACT.Tanh, scale=2.0).then_inc(s["tanh"], 1)

            def np_(u):
                act.wait_ge(s["scales"], u + 1)
                if u >= 3:
                    act.wait_ge(s["traj_ps"], u - 2)
                for k in range(NT):
                    act.activation(V[u % 3][:, k, 0:D], Dd[u % 3][:, k // 2, k % 2, :], ACT.Identity, scale=st[u % 3][:, CN, k:k + 1])
                act.activation(V[u % 3][:, :, D], st[u % 3][:, MT, :], ACT.Identity).then_inc(s["np"], 1)

            def nT_(u):
                act.wait_ge(s["nT_ps"], u + 1)
                if u >= 1:
                    act.wait_ge(s["sims_ps"], u)
                act.activation(nT[:, :], nT_ps[:, :], ACT.Identity).then_inc(s["nT_sb"], 1)

            def et(u):
                act.wait_ge(s["sims_ps"], u + 1)
                if u >= 2:
                    act.wait_ge(s["infl_ps"], u - 1)
                act.activation(ET[u % 2][:, :], sims_ps[0:G, :], ACT.Exp, scale=2.0).then_inc(s["ET"], 1)

            def x1(u):
                act.wait_ge(s["x1c"], u + 1)
                if u >= 4:
                    act.wait_ge(scattered[u % 4], 16 * NT * (u // 4))
                for k in range(NT):
                    a = act.activation(R[u % 4][:, k, 0:D], Y[u % 2][:, k, :], ACT.Identity,
                                       scale=rstd[u % 2][:, k:k + 1], bias=st[u % 3][:, WR, k:k + 1])
                a.then_inc(s["x1"], 1)

            def xT_(u):
                act.wait_ge(s["xT_ps"], u + 1)
                if u >= 1:
                    act.wait_ge(s["logits_ps"], u)
                act.activation(xT[:, :], xT_ps[:, :], ACT.Identity).then_inc(s["xT_sb"], 1)

            def rexp(u):
                act.wait_ge(s["shifted"], u + 1)
                act.activation(ex[:, :, :], lg[:, :, :], ACT.Exp).then_inc(s["exped"], 1)

            def weights_hi(q):
                act.wait_ge(s["scales_w"], 1)
                e = 2 * q
                act.activation(W1h[:, e * FF:(e + 2) * FF], W1[:, e:e + 2, :], ACT.Identity, scale=scl[:, 1:2])
                act.activation(W2hl[:, e * FC:(e + 2) * FC, 0:D], W2[:, e:e + 2, :, :], ACT.Identity,
                               scale=scl[:, 2:3]).then_inc(s["split_hi"], 1)

            for i in range(-2, NU + 3):
                if 0 <= i < NU:
                    nT_(i)
                if i >= NU - 1:
                    weights_hi(i - NU + 1)
                if 0 <= i < NU:
                    et(i)
                if i >= 3:
                    rexp(i - 3)
                if 0 <= i + 1 < NU:
                    tanh(i + 1)
                if 2 <= i <= NU + 1:
                    x1(i - 2)
                if i + 2 < NU:
                    sumsq(i + 2)
                if 2 <= i <= NU + 1:
                    xT_(i - 2)
                if 0 <= i + 1 < NU:
                    np_(i + 1)
                if i == 7:
                    act.activation(bias3[:, :], bias[:, :], ACT.Identity).then_inc(s["bias_hi"], 1)
                if i == 8:
                    act.wait_ge(s["bias_rest"], 1)
                    act.activation(bias_m[:, :], bias_r[:, :], ACT.Identity)
                    act.activation(bias3[32:64, :], bias_r[32:64, :], ACT.Identity).then_inc(s["bias_hi"], 1)

            act.wait_ge(s["pad_rows"], 1)
            pads(act, E // 2, E // 2)
            act.activation(warm[:, 1:2], epsc[:, :], ACT.Sqrt)

            def b_xs(count, k):
                act.wait_ge(row_loaded[k], count(1) * 16)
                act.activation(xs[k][:, :], XR[k][:, 0:D], ACT.Identity, scale=XR[k][:, D + 1:D + 2]).then_inc(t["xs"][k], 1)

            def b_xt(count, k):
                act.wait_ge(every["xT_ps"], blocks(count(0), k))
                act.activation(xt[k][:, :], bank[7 * (k % 2)][:, 0:P], ACT.Identity, scale=gbs[:, 0:1], bias=gbs[:, 1:2]).then_inc(every["xt"], 1)

            def b_xh(count, k):
                act.wait_ge(every["xt"], blocks(count(0), k))
                act.activation(xh[k][:, :], xt[k][:, :], ACT.Identity).then_inc(t["xh"][k], 1)

            def b_hh(count, k):
                act.wait_ge(every["token"], blocks(count(0), k))
                act.wait_ge(every["h_ps"], blocks(count(0), k))
                act.activation(hh[k][:, :], bank[1 + k % 4][:, :], ACT.Relu).then_inc(every["hh"], 1)

            def b_sd(count, k):
                after(act, stored[k], count(0) * 16)
                act.wait_ge(every["mv"], blocks(count(0), k))
                act.activation(sd[k][:, 0:1], mv2[k][:, 1:2], ACT.Sqrt, bias=epsc[:, 0:1]).then_inc(every["sd"], 1)

            def b_fin(count, k):
                act.wait_ge(every["shift"], blocks(count(0), k))
                act.activation(OUT[k][:, :], z[k][:, :], ACT.Identity, scale=sd[k][:, 1:2], bias=sd[k][:, 2:3]).then_inc(every["out"], 1)

            steps(act, [(5, b_xs), (1, b_hh), (-3, b_fin), (4, b_xt), (-2, b_sd), (4, b_xh)])

        @block.vector
        def _(dve):
            tt, ts, stt = dve.tensor_tensor, dve.tensor_scalar, dve.scalar_tensor_tensor

            dve.wait_ge(ld["guide"], 16)
            dve.wait_ge(s["zeroed"], 1)
            tt(gdn[:, :], gd[:, :], gd[:, :], ALU.mult)
            ts(gdz[:, 0:D], gd[:, :], GUIDE, None, ALU.mult)
            dve.drain()
            dve.tensor_reduce(gst[:, 0:1], gdn[:, :], AX.X, ALU.add).then_inc(s["guide_sq"], 1)

            def guide():
                dve.wait_ge(s["guide_norm"], 1)
                ts(gdn[:, :], gd[:, :], gst[:, 2:3], None, ALU.mult).then_inc(s["guided"], 1)
                dve.wait_ge(ld["cst"], 16)
                dve.tensor_copy(lt16[:, :], C[:, C_LT:C_LT + P])
                dve.wait_ge(s["guideT_ps"], 1)
                dve.tensor_copy(gdT[:, :], log_ps[:, 128:128 + G]).then_inc(s["guideT"], 1)

            def diff(u):
                g = [0, 1, 1, 2, 2, 3, 3, 3][u]
                dve.wait_ge(ld[f"x{g}"], 32 if g < 3 else 64)
                if u >= 3:
                    dve.wait_ge(s["np"], u - 2)
                b = slice(2 * u, 2 * u + 2)
                tt(Dd[u % 3][:, :, 0, :], X[:, b, 1, :], X[:, b, 0, :], ALU.subtract)
                tt(Dd[u % 3][:, :, 1, :], XN[:, b, :], X[:, b, 1, :], ALU.subtract).then_inc(s["diff"], 1)

            def window(i):
                v, y, r, g = i - 1, i - 2, i - 3, i - 4
                do_v, do_y, do_r, do_g = 0 <= v < NU, 0 <= y < NU, 0 <= r < NU, 0 <= g < NU
                sv, sy = st[v % 3], st[y % 3]
                if do_g:
                    dve.tensor_reduce(cnt[:, :], oh[:, :, :].rearrange("p k e -> p e k"), AX.X, ALU.add)
                    dve.wait_ge(s["exped"], g + 1)
                    dve.tensor_reduce(rt[:, 2, :], ex[:, :, :], AX.X, ALU.add)
                    dve.wait_ge(s["rank_ps"], g + 1)
                    tt(pl[:, :, :], rank_ps.rearrange("p (k e) -> p k e", k=NT), C[:, C_REG:C_REG + E].unsqueeze(1).to_broadcast([P, NT, E]), ALU.add)
                if do_y:
                    dve.wait_ge(s["traj_ps"], y + 1)
                    for h in range(2):
                        ts(sy[:, WI, 2 * h:2 * h + 2].unsqueeze(2), pair(traj_ps[h])[:, :, D:D + 1], EPS_WSUM, None, ALU.max)
                if do_v:
                    dve.wait_ge(s["infl_ps"], v + 1)
                    for h in range(2):
                        dve.reciprocal(sv[:, ZI, 2 * h:2 * h + 2].unsqueeze(2), pair(infl_ps[h])[:, :, D:D + 1])
                if i == 6:
                    scales(0)
                dve.drain()
                if do_y:
                    dve.reciprocal(sy[:, SS, :], sy[:, WI, :])
                if do_v:
                    tt(sv[:, Q, :], sv[:, ZI, :], sv[:, MT, :], ALU.mult)
                if do_g:
                    if g >= 4:
                        dve.wait_ge(scattered[g % 4], 16 * NT * (g // 4))
                    tt(pl[:, :, :], pl[:, :, :], oh[:, :, :], ALU.mult)
                    dve.reciprocal(R[g % 4][:, :, D], rt[:, 2, :])
                    tt(carry[:, :], carry[:, :], cnt[:, :], ALU.add)
                if i == 6:
                    scales(1)
                dve.drain()
                if do_v:
                    dve.wait_ge(s["np"], v + 1)
                    for k in range(NT):
                        a = stt(V[v % 3][:, k, 0:D], tile_of(infl_ps, k)[:, 0:D], sv[:, Q, k:k + 1], V[v % 3][:, k, 0:D], ALU.mult, ALU.add)
                    a.then_inc(s["V"], 1)
                if do_y:
                    if y >= 2:
                        dve.wait_ge(s["x1"], y - 1)
                    for k in range(NT):
                        a = stt(Y[y % 2][:, k, :], tile_of(traj_ps, k)[:, 0:D], sy[:, SS, k:k + 1], X[:, 2 * y + k // 2, k % 2, :],
                                ALU.mult, ALU.add)
                    a.then_inc(s["y"], 1)
                if do_g:
                    dve.tensor_reduce(rt[:, 3, :], pl[:, :, :], AX.X, ALU.add)
                    dve.tensor_copy(carry16[:, :], carry[:, :]).then_inc(s["counted"], 1)
                if i == 6:
                    scales(2)
                dve.drain()
                if do_g:
                    dve.tensor_copy(place[g % 4][:, :], rt[:, 3, :]).then_inc(s["placed"], 1)
                if do_y:
                    for k in range(NT):
                        dve.bn_stats(bn[:, k, :], Y[y % 2][:, k, :])
                if do_r:
                    dve.wait_ge(s["logits_ps"], r + 1)
                    if r == 0:
                        dve.wait_ge(ld["small"], 64)
                    tt(lg[:, :, :], log_ps[:, 0:NT * E].rearrange("p (k e) -> p k e", k=NT), brb[:, :].unsqueeze(1).to_broadcast([P, NT, E]), ALU.add)
                if i == 6:
                    scales(3)
                dve.drain()
                if do_y:
                    for k in range(NT):
                        dve.bn_aggr(mv[y % 2][:, k, :], bn[:, k, :])
                if do_r:
                    dve.tensor_reduce(rt[:, 0, :], lg[:, :, :], AX.X, ALU.max)
                if i == 6:
                    scales(4)
                dve.drain()
                if do_y:
                    ts(var_in[y % 2][:, 0, :], mv[y % 2][:, :, 1], LN_EPS, None, ALU.add).then_inc(s["var_in"], 1)
                if do_r:
                    tt(lg[:, :, :], lg[:, :, :], rt[:, 0, :].unsqueeze(2).to_broadcast([P, NT, E]), ALU.subtract).then_inc(s["shifted"], 1)
                if i == 6:
                    scales(5)
                dve.drain()
                if do_y:
                    dve.reciprocal(sy[:, RV, :], var_in[y % 2][:, 0, :])
                if do_r:
                    stt(oh[:, :, :], lg[:, :, :], 0.0, C[:, C_REV:C_REV + E].unsqueeze(1).to_broadcast([P, NT, E]), ALU.is_ge, ALU.mult)
                if i == 6:
                    scales(6)
                dve.drain()
                if do_y:
                    tt(sy[:, VP, :], mv[y % 2][:, :, 1], sy[:, RV, :], ALU.mult)
                if do_r:
                    dve.tensor_reduce(rt[:, 1, :], oh[:, :, :], AX.X, ALU.max)
                if i == 6:
                    scales(7)
                dve.drain()
                if do_y:
                    ts(var_in[y % 2][:, 1, :], sy[:, VP, :], LN_EPS, None, ALU.add).then_inc(s["var2_in"], 1)
                if do_r:
                    tt(oh[:, :, :], oh[:, :, :], rt[:, 1, :].unsqueeze(2).to_broadcast([P, NT, E]), ALU.is_equal)
                if i == 6:
                    scales(8)
                dve.drain()
                if do_r:
                    dve.tensor_copy(oh16[:, :, :], oh[:, :, :]).then_inc(s["onehot"], 1)
                if i == 6:
                    scales(9)

            def factors(i):
                u, y = i + 1, i - 2
                m, r = st[u % 3], rmag[u % 2]
                if 0 <= u < NU:
                    dve.wait_ge(s["rmag"], u + 1)
                    tt(m[:, MAG, :], sumsq_in[u % 2][:, :], r[:, :], ALU.mult)
                    dve.drain()
                    stt(m[:, INV, :], m[:, MAG, :], EPS_MAG, r[:, :], ALU.is_gt, ALU.mult).then_inc(s["mags"], 1)
                if 0 <= y < NU:
                    dve.wait_ge(s["rstd"], y + 1)
                    stt(st[y % 3][:, WR, :], mv[y % 2][:, :, 0], -1.0, rstd[y % 2][:, :], ALU.mult, ALU.mult).then_inc(s["x1c"], 1)

            def directions(u):
                dve.drain()
                if u >= 2:
                    dve.wait_ge(s["nT_ps"], u - 1)
                for k in range(NT):
                    a = ts(N[u % 2][:, k, :], Dd[u % 3][:, k // 2, k % 2, :], st[u % 3][:, INV, k:k + 1], None, ALU.mult)
                a.then_inc(s["n"], 1)
                dve.wait_ge(s["tanh"], u + 1)
                stt(st[u % 3][:, CN, :], st[u % 3][:, MT, :], 1.0 - GUIDE, st[u % 3][:, INV, :], ALU.mult, ALU.mult).then_inc(s["scales"], 1)

            def maxima1(q):
                if q == 0:
                    dve.wait_ge(ld["w1"], 16)
                dve.tensor_reduce(mx[:, 4 + q:5 + q], W1[:, 2 * q:2 * q + 2, :], AX.XY, ALU.max, apply_absolute_value=True)

            def maxima2(q):
                if q == 0:
                    dve.wait_ge(ld["w2"], 16)
                dve.tensor_reduce(mx[:, 8 + q:9 + q], W2[:, 2 * q:2 * q + 2, :, :], AX.XYZ, ALU.max, apply_absolute_value=True)
                if q == 3:
                    dve.wait_ge(ld["bias"], 96)
                    dve.drain()
                    stt(mx[:, 12:14], gb[:, :], -1.0, gb[:, :], ALU.mult, ALU.max)
                    dve.tensor_reduce(mx[:, 1:2], mx[:, 4:8], AX.X, ALU.max)
                    dve.tensor_reduce(mx[:, 2:3], mx[:, 8:12], AX.X, ALU.max)
                    dve.tensor_reduce(mx[0:96, 3:4], bias[:, 0:FF], AX.X, ALU.max, apply_absolute_value=True)
                    dve.drain()
                    stt(mx[:, 0:1], mx[:, 12:13], 11.5, mx[:, 13:14], ALU.mult, ALU.add).then_inc(s["maxima"], 1)

            def power(dst, src, k, second):
                if second:
                    return ts(dst.bitcast(I32), dst.bitcast(I32), -1.0, float((254 + k) << 23), ALU.mult, ALU.add)
                return ts(dst.bitcast(I32), src.bitcast(I32), POW2_MASK, None, ALU.bitwise_and)

            def scales(step):
                v = scl[:, 8:12]
                if step == 0:
                    power(scl[:, 0:1], v[:, 0:1], 5, False)
                    power(scl[:, 2:3], v[:, 2:3], 8, False)
                elif step == 1:
                    power(scl[:, 0:1], v[:, 0:1], 5, True)
                    power(scl[:, 2:3], v[:, 2:3], 8, True)
                elif step == 2:
                    tt(scl[:, 12:13], v[:, 3:4], scl[:, 0:1], ALU.mult)
                    ts(scl[:, 13:14], v[:, 1:2], 0.5, None, ALU.mult)
                elif step == 3:
                    stt(scl[:, 14:15], scl[:, 12:13], 2.0 ** -13, scl[:, 13:14], ALU.mult, ALU.max)
                elif step == 4:
                    power(scl[:, 1:2], scl[:, 14:15], 0, False)
                elif step == 5:
                    power(scl[:, 1:2], scl[:, 14:15], 0, True)
                elif step == 6:
                    tt(scl[:, 4:5], scl[:, 0:1], scl[:, 1:2], ALU.mult)
                    ts(gbs[:, :], gb[:, :], scl[:, 0:1], None, ALU.mult)
                elif step == 7:
                    tt(scl[:, 5:6], scl[:, 4:5], scl[:, 2:3], ALU.mult)
                    ts(bias[:, 0:FF], bias[:, 0:FF], scl[0:96, 4:5], None, ALU.mult)
                elif step == 8:
                    power(scl[:, 3:4], scl[:, 5:6], 0, False)
                    ts(bias[:, FF:FF + D], bias[:, FF:FF + D], scl[0:96, 5:6], None, ALU.mult)
                elif step == 9:
                    power(scl[:, 3:4], scl[:, 5:6], 0, True).then_inc(s["scales_w"], 1)

            def split_bias(piece):
                if piece == 0:
                    dve.wait_ge(s["bias_hi"], 1)
                    tt(bias_r[:, :], bias[:, :], bias3[:, :], ALU.subtract).then_inc(s["bias_rest"], 1)
                else:
                    dve.wait_ge(s["bias_hi"], 2)
                    tt(bias3[64:96, :], bias_r[64:96, :], bias_m[64:96, :], ALU.subtract)

            def split_lo(q):
                dve.wait_ge(s["split_hi"], q + 1)
                e2 = slice(2 * q * FF, (2 * q + 2) * FF)
                stt(W1l[:, e2].rearrange("p (e f) -> p e f", e=2), W1[:, 2 * q:2 * q + 2, :], scl[:, 1:2],
                    W1h[:, e2].rearrange("p (e f) -> p e f", e=2), ALU.mult, ALU.subtract)
                w = W2hl[:, 2 * q * FC:(2 * q + 2) * FC, :]
                stt(w[:, :, D:2 * D], W2[:, 2 * q:2 * q + 2, :, :].rearrange("p e c d -> p (e c) d"), scl[:, 2:3], w[:, :, 0:D], ALU.mult, ALU.subtract)

            for i in range(-2, NU + 4):
                if i == 5:
                    dve.wait_ge(s["maxT_ps"], 1)
                    dve.tensor_reduce(mx4[:, 4:5], xT_ps[0:4, 0:P], AX.X, ALU.max)
                    dve.drain()
                    ts(mx4[:, 0:4], ident[0:4, 0:4], mx4[:, 4:5], None, ALU.mult).then_inc(s["max4"], 1)
                if i >= 1:
                    window(i)
                if i + 2 < NU:
                    diff(i + 2)
                if i == -2:
                    guide()
                if i >= -1:
                    factors(i)
                if 2 <= i < 5:
                    maxima2(i - 2)
                if i == 4:
                    maxima2(3)
                if i == 5:
                    dve.wait_ge(s["maxb_ps"], 1)
                    ts(scl[:, 8:12], xT_ps[:, P:P + 4], 2.0 ** -40, None, ALU.max).then_inc(s["max_read"], 1)
                if 8 <= i <= 9:
                    split_bias(i - 8)
                if i in LO_AT:
                    split_lo(LO_AT.index(i))
                if 0 <= i + 1 < NU:
                    directions(i + 1)
                if 0 <= i < 2:
                    maxima1(2 * i)
                    maxima1(2 * i + 1)

            dve.wait_ge(s["tot_ps"], 1)
            dve.tensor_copy(tot[:, :], log_ps[:, 300:300 + E])
            dve.drain()
            ts(nblk_i[:, :], tot[:, :], float(P - 1), None, ALU.add)
            tt(pad_row[:, :], tot[:, :], C[:, C_REG:C_REG + E], ALU.add)
            dve.drain()
            ts(nblk_i[:, :], nblk_i[:, :], 7, None, ALU.arith_shift_right)
            dve.drain().then_inc(s["pad_rows"], 1)
            dve.tensor_copy(nblk[:, :], nblk_i[:, :])
            dve.drain()
            dve.tensor_tensor_scan(cend[:, :], ones[:, 0:E], nblk[:, :], 0.0, ALU.mult, ALU.add)
            ts(jump[:, :], nblk[:, :], -float(P), float(REG), ALU.mult, ALU.add)
            dve.drain()
            tt(past[:, :, :], cend[:, :].unsqueeze(1).to_broadcast([P, NB, E]),
               C[:, C_BLK:C_BLK + NB].unsqueeze(2).to_broadcast([P, NB, E]), ALU.is_le)
            dve.drain()
            dve.tensor_reduce(blk[:, 0, :], past[:, :, :], AX.X, ALU.add)
            tt(past2[:, :, :], past[:, :, :], jump[:, :].unsqueeze(1).to_broadcast([P, NB, E]), ALU.mult)
            dve.drain()
            dve.tensor_reduce(blk[:, 1, :], past2[:, :, :], AX.X, ALU.add)
            ts(blk[:, 0, :], blk[:, 0, :], float(E - 1), None, ALU.min)
            dve.drain()
            stt(blk[:, 2, :], C[:, C_BLK:C_BLK + NB], float(P), blk[:, 1, :], ALU.mult, ALU.add)
            dve.tensor_copy(blk_e[:, 0:NB], blk[:, 0, :])
            ts(sel16[:, :], blk[0:96, 0, :], C[0:96, C_EID:C_EID + 1], None, ALU.is_equal)
            dve.drain()
            ts(blk_row[:, 0:NB], blk[:, 2, :], float(PADROW), None, ALU.min)
            dve.drain().then_inc(s["table"], 1)
            for q in range(len(LO_AT), E // 2):
                split_lo(q)
            dve.drain().then_inc(s["split_lo"], 1)

            def b_xl(count, k):
                dve.wait_ge(t["xh"][k], count(1))
                tt(xl[k][:, :], xt[k][:, :], xh[k][:, :], ALU.subtract).then_inc(t["xl"][k], 1)

            def b_hl(count, k):
                j = (k - 2) % UN
                after(dve, every["bn"], blocks(count((k - 2) // UN), j))
                dve.wait_ge(every["hh"], blocks(count(0), k))
                stt(hl[k][:, :], bank[1 + k % 4][:, :], 0.0, hh[k][:, :], ALU.max, ALU.subtract).then_inc(t["hl"][k], 1)

            def b_z0(count, k):
                dve.wait_ge(every["y_ps"], blocks(count(0), k))
                stt(z0[k][:, :], bank[5 + k % 2][:, 0:D], cg[k][:, :], XR[k][:, 0:D], ALU.mult, ALU.add).then_inc(every["z0"], 1)

            def b_z(count, k):
                dve.wait_ge(every["z0"], blocks(count(0), k))
                stt(z[k][:, :], bank[5 + k % 2][:, D:2 * D], cg[k][:, :], z0[k][:, :], ALU.mult, ALU.add).then_inc(t["z"][k], 1)

            def b_bn(count, k):
                dve.wait_ge(t["z"][k], count(1))
                dve.bn_stats(bn2[k][:, :], z[k][:, :]).then_inc(every["bn"], 1)

            def b_mv(count, k):
                if isinstance(count(0), int):
                    dve.wait_ge(every["bn"], blocks(count(0), k))
                dve.bn_aggr(mv2[k][:, :], bn2[k][:, :]).then_inc(every["mv"], 1)

            def b_rec(count, k):
                dve.wait_ge(every["sd"], blocks(count(0), k))
                dve.reciprocal(sd[k][:, 1:2], sd[k][:, 0:1]).then_inc(every["rec"], 1)

            def b_shift(count, k):
                dve.wait_ge(every["rec"], blocks(count(0), k))
                stt(sd[k][:, 2:3], mv2[k][:, 0:1], -1.0, sd[k][:, 1:2], ALU.mult, ALU.mult).then_inc(every["shift"], 1)

            steps(dve, [(1, b_hl), (-1, b_mv), (0, b_z0), (-2, b_rec), (0, b_z), (-2, b_shift), (0, b_bn), (4, b_xl)])


def kernel(**inputs):
    import concourse.bacc as bacc
    from concourse.bass_utils import run_bass_kernel_spmd

    nc = bacc.Bacc("TRN2", target_bir_lowering=False, num_devices=1)
    arrays, aps = {}, []
    names = ("attn_embeddings", "attn_guidance_trajectories", "ffn_Wr", "ffn_br", "ffn_ln_g", "ffn_ln_b",
             "ffn_W1", "ffn_b1", "ffn_W2", "ffn_b2")
    for name in names:
        a = np.ascontiguousarray(inputs["L0_" + name])
        arrays["in_" + name] = a
        aps.append(nc.dram_tensor("in_" + name, a.shape, mybir.dt.from_np(a.dtype), kind="ExternalInput").ap())
    arrays["in_constants"] = constants()
    aps.append(nc.dram_tensor("in_constants", (P, C_N), F32, kind="ExternalInput").ap())
    rows = nc.dram_tensor("rows", (PADROW + P, ROW), F32, kind="Internal").ap()
    out = nc.dram_tensor("out", (T, D), F32, kind="ExternalOutput").ap()
    build(nc, *aps, rows, out)
    r = run_bass_kernel_spmd(nc, [arrays], core_ids=[0])
    return r.results[0]["out"].reshape(B, S, D)
```
